# Optimizing a Trainium2 kernel written in Bass

```python
import numpy as np
import jax
import jax.numpy as jnp

def _softmax(x, axis=-1):
    return jax.nn.softmax(x, axis=axis)

def _gelu(x):
    return jax.nn.gelu(x, approximate=True)

def _silu(x):
    return jax.nn.silu(x)

def _sigmoid(x):
    return jax.nn.sigmoid(x)

def _layernorm(x, axis=-1, eps=1e-05):
    m = jnp.mean(x, axis=axis, keepdims=True)
    v = jnp.var(x, axis=axis, keepdims=True)
    return (x - m) / jnp.sqrt(v + eps)

def _scatter_add(tgt, idx, src, axis=0):
    return tgt.at[idx].add(src)

def _segment_sum(src, seg, n):
    return jax.ops.segment_sum(src, seg, n)
kernel_name = 'mk_decoder_preln_d4_seqx_r8_93bf23'

def setup_inputs(seed: int=0):
    np.random.seed(seed)
    _w = jnp.asarray

    def _rec_inputs():
        import jax
        import jax.numpy as jnp
        _rk = jax.random.key(seed)
        x = -0.0002928 + 1 * jax.random.normal(jax.random.fold_in(_rk, 1), (64, 64, 128), jnp.float32)
        _lenS = 64 - jax.random.randint(jax.random.fold_in(_rk, 7), (64,), 0, max(1, 64 // 4) + 1, jnp.int32)
        _lenS2 = 64 - jax.random.randint(jax.random.fold_in(_rk, 8), (64,), 0, max(1, 64 // 4) + 1, jnp.int32)
        _ctx_1024P = jax.random.normal(jax.random.fold_in(_rk, 11), (64, 16, 128), jnp.float32)
        _ctx_1024c = jax.random.dirichlet(jax.random.fold_in(_rk, 511), 0.3 * jnp.ones((16,), jnp.float32), (64, 64))
        _ctx_1024t = jnp.einsum('bsk,bkd->bsd', _ctx_1024c, _ctx_1024P)
        _ctx_1024t = _ctx_1024t * jax.lax.rsqrt(jnp.mean(jnp.square(_ctx_1024t)) + 1e-12) * 0.953939
        ctx_1024 = -1.39393e-06 + 0.999914 * (_ctx_1024t + 0.3 * jax.random.normal(jax.random.fold_in(_rk, 611), (64, 64, 128), jnp.float32))
        return (x, ctx_1024)
    x, ctx_1024 = _rec_inputs()

    def _L0_attn_setup():
        import jax, jax.numpy as jnp
        import numpy as np
        B, T, D = (4, 256, 128)

        def ste_sign(x):
            return jax.lax.stop_gradient(jnp.sign(x) - x) + x
        key = jax.random.key(seed)
        kx, kq, kk, kv = jax.random.split(key, 4)
        return {'x': jax.random.normal(kx, (B, T, D), dtype=jnp.float32), 'bv_q': jax.random.normal(kq, (D,), dtype=jnp.float32) * 0.02, 'bv_k': jax.random.normal(kk, (D,), dtype=jnp.float32) * 0.02, 'bv_v': jax.random.normal(kv, (D,), dtype=jnp.float32) * 0.02}
    _L0_attn_all = _L0_attn_setup()
    _L0_attn_in = {k: v for k, v in _L0_attn_all.items() if k in ('bv_q', 'bv_k', 'bv_v')}
    del _L0_attn_all

    def _L0_xattn_setup():
        import jax, jax.numpy as jnp
        import numpy as np
        D_MODEL = 128
        NUM_HEADS = 16
        D_K = D_MODEL // NUM_HEADS
        LN_EPS = 1e-05

        def _layernorm(x, gamma, beta):
            mu = jnp.mean(x, axis=-1, keepdims=True)
            var = jnp.var(x, axis=-1, keepdims=True)
            return (x - mu) * jax.lax.rsqrt(var + LN_EPS) * gamma + beta
        key = jax.random.key(seed)
        ks = jax.random.split(key, 7)
        B, S = (2, 256)
        scale = 1.0 / np.sqrt(D_MODEL)
        return {'query': jax.random.normal(ks[0], (B, S, D_MODEL), jnp.float32), 'key': jax.random.normal(ks[1], (B, S, D_MODEL), jnp.float32), 'value': jax.random.normal(ks[2], (B, S, D_MODEL), jnp.float32), 'Wq': jax.random.normal(ks[3], (D_MODEL, D_MODEL), jnp.float32) * scale, 'Wk': jax.random.normal(ks[4], (D_MODEL, D_MODEL), jnp.float32) * scale, 'Wv': jax.random.normal(ks[5], (D_MODEL, D_MODEL), jnp.float32) * scale, 'Wo': jax.random.normal(ks[6], (D_MODEL, D_MODEL), jnp.float32) * scale, 'ln_gamma': jnp.ones((D_MODEL,), jnp.float32), 'ln_beta': jnp.zeros((D_MODEL,), jnp.float32)}
    _L0_xattn_all = _L0_xattn_setup()
    _L0_xattn_in = {k: v for k, v in _L0_xattn_all.items() if k in ('Wq', 'Wk', 'Wv', 'Wo', 'ln_gamma', 'ln_beta')}
    del _L0_xattn_all

    def _L0_ffn_setup():
        import jax, jax.numpy as jnp
        import numpy as np
        B, T, C = (2, 64, 128)
        I = 512
        E = 8
        K = 2
        key = jax.random.key(seed)
        ks = jax.random.split(key, 8)
        s = 0.02
        return {'x': jax.random.normal(ks[0], (B, T, C), jnp.float32), 'Wr1': jax.random.normal(ks[1], (C, C // 4), jnp.float32) * s, 'br1': jnp.zeros((C // 4,), jnp.float32), 'Wr2': jax.random.normal(ks[2], (C // 4, E), jnp.float32) * s, 'br2': jnp.zeros((E,), jnp.float32), 'Ws1': jax.random.normal(ks[3], (C, I), jnp.float32) * s, 'bs1': jnp.zeros((I,), jnp.float32), 'Ws2': jax.random.normal(ks[4], (I, C), jnp.float32) * s, 'bs2': jnp.zeros((C,), jnp.float32), 'We1': jax.random.normal(ks[5], (E, C, I), jnp.float32) * s, 'be1': jnp.zeros((E, I), jnp.float32), 'We2': jax.random.normal(ks[6], (E, I, C), jnp.float32) * s, 'be2': jnp.zeros((E, C), jnp.float32)}
    _L0_ffn_all = _L0_ffn_setup()
    _L0_ffn_in = {k: v for k, v in _L0_ffn_all.items() if k in ('Wr1', 'br1', 'Wr2', 'br2', 'Ws1', 'bs1', 'Ws2', 'bs2', 'We1', 'be1', 'We2', 'be2')}
    del _L0_ffn_all

    def _L1_attn_setup():
        import jax, jax.numpy as jnp
        import numpy as np
        B, N, H = (4, 512, 128)
        NUM_HEADS = 16
        HEAD_DIM = H // NUM_HEADS
        EPS = 1e-05

        def _layernorm(x, g, b):
            mu = jnp.mean(x, axis=-1, keepdims=True)
            var = jnp.mean(jnp.square(x - mu), axis=-1, keepdims=True)
            return (x - mu) * jax.lax.rsqrt(var + EPS) * g + b
        key = jax.random.key(seed)
        ks = jax.random.split(key, 12)
        s = 0.02
        return {'x': jax.random.normal(ks[0], (B, N, H), dtype=jnp.float32), 'w_qkv': jax.random.normal(ks[1], (3 * H, H), dtype=jnp.float32) * s, 'b_qkv': jax.random.normal(ks[2], (3 * H,), dtype=jnp.float32) * s, 'w_g1': jax.random.normal(ks[3], (HEAD_DIM, H), dtype=jnp.float32) * s, 'b_g1': jax.random.normal(ks[4], (HEAD_DIM,), dtype=jnp.float32) * s, 'w_g2': jax.random.normal(ks[5], (H, HEAD_DIM), dtype=jnp.float32) * s, 'b_g2': jax.random.normal(ks[6], (H,), dtype=jnp.float32) * s, 'w_out': jax.random.normal(ks[7], (H, H), dtype=jnp.float32) * s, 'b_out': jax.random.normal(ks[8], (H,), dtype=jnp.float32) * s, 'ln_g': jnp.ones((H,), dtype=jnp.float32), 'ln_b': jnp.zeros((H,), dtype=jnp.float32)}
    _L1_attn_all = _L1_attn_setup()
    _L1_attn_in = {k: v for k, v in _L1_attn_all.items() if k in ('w_qkv', 'b_qkv', 'w_g1', 'b_g1', 'w_g2', 'b_g2', 'w_out', 'b_out', 'ln_g', 'ln_b')}
    del _L1_attn_all

    def _L1_xattn_setup():
        import jax, jax.numpy as jnp
        import numpy as np
        EMBED_DIM = 128
        B, QL, KL = (4, 256, 256)
        key = jax.random.key(seed)
        k1, k2, k3, k4 = jax.random.split(key, 4)
        hidden_states = jax.random.normal(k1, (B, QL, EMBED_DIM), dtype=jnp.float32)
        decoder_hidden_states = jax.random.normal(k2, (B, KL, EMBED_DIM), dtype=jnp.float32)
        Wq = jax.random.normal(k3, (EMBED_DIM, EMBED_DIM), dtype=jnp.float32) * (1.0 / np.sqrt(EMBED_DIM))
        Wkv = jax.random.normal(k4, (EMBED_DIM, 2 * EMBED_DIM), dtype=jnp.float32) * (1.0 / np.sqrt(EMBED_DIM))
        return {'hidden_states': hidden_states, 'decoder_hidden_states': decoder_hidden_states, 'Wq': Wq, 'Wkv': Wkv}
    _L1_xattn_all = _L1_xattn_setup()
    _L1_xattn_in = {k: v for k, v in _L1_xattn_all.items() if k in ('Wq', 'Wkv')}
    del _L1_xattn_all

    def _L1_ffn_setup():
        import jax, jax.numpy as jnp
        import numpy as np
        D_MODEL = 128
        DEPTH = 8
        M = 2 ** DEPTH
        N_INTERNAL = M - 1
        B, T = (8, 512)

        def _leaf_probs(gate):
            BT = gate.shape[0]
            lp = jnp.ones((BT, M), dtype=gate.dtype)
            for level in range(DEPTH):
                n = 2 ** level
                half = M // (2 * n)
                g = gate[:, n - 1:2 * n - 1]
                f = jnp.stack([1.0 - g, g], axis=-1)
                f = jnp.broadcast_to(f[..., None], (BT, n, 2, half))
                lp = lp * f.reshape(BT, M)
            return lp
        key = jax.random.key(seed)
        ks = jax.random.split(key, 7)
        x = jax.random.normal(ks[0], (B, T, D_MODEL), dtype=jnp.float32)
        Wq = jax.random.normal(ks[1], (D_MODEL, D_MODEL), dtype=jnp.float32) * 0.02
        routers = jax.random.normal(ks[2], (N_INTERNAL, D_MODEL), dtype=jnp.float32) * 0.02
        leaf_keys = jax.random.normal(ks[3], (M, D_MODEL), dtype=jnp.float32) * 0.02
        leaf_values = jax.random.normal(ks[4], (M, D_MODEL), dtype=jnp.float32) * 0.02
        Wout_w = jax.random.normal(ks[5], (D_MODEL, D_MODEL), dtype=jnp.float32) * 0.02
        Wout_b = jax.random.normal(ks[6], (D_MODEL,), dtype=jnp.float32) * 0.02
        return {'x': x, 'Wq': Wq, 'routers': routers, 'leaf_keys': leaf_keys, 'leaf_values': leaf_values, 'Wout_w': Wout_w, 'Wout_b': Wout_b}
    _L1_ffn_all = _L1_ffn_setup()
    _L1_ffn_in = {k: v for k, v in _L1_ffn_all.items() if k in ('Wq', 'routers', 'leaf_keys', 'leaf_values', 'Wout_w', 'Wout_b')}
    del _L1_ffn_all

    def _L2_attn_setup():
        import jax, jax.numpy as jnp
        import numpy as np
        B, N, QD = (4, 512, 128)
        HEADS, DIM_HEAD = (8, 64)
        HID = HEADS * DIM_HEAD
        SCALE = DIM_HEAD ** (-0.5)
        key = jax.random.key(seed)
        ks = jax.random.split(key, 6)
        s_in = 1.0 / np.sqrt(QD)
        s_h = 1.0 / np.sqrt(HID)
        return {'x': jax.random.normal(ks[0], (B, N, QD), dtype=jnp.float32), 'Wq': jax.random.uniform(ks[1], (QD, HID), jnp.float32, -s_in, s_in), 'Wk': jax.random.uniform(ks[2], (QD, HID), jnp.float32, -s_in, s_in), 'Wv': jax.random.uniform(ks[3], (QD, HID), jnp.float32, -s_in, s_in), 'Wo': jax.random.uniform(ks[4], (HID, QD), jnp.float32, -s_h, s_h), 'bo': jax.random.uniform(ks[5], (QD,), jnp.float32, -s_h, s_h)}
    _L2_attn_all = _L2_attn_setup()
    _L2_attn_in = {k: v for k, v in _L2_attn_all.items() if k in ('Wq', 'Wk', 'Wv', 'Wo', 'bo')}
    del _L2_attn_all

    def _L2_xattn_setup():
        import jax, jax.numpy as jnp
        import numpy as np
        B, S, E, NH = (1, 256, 128, 8)
        DH = E // NH
        EPS_BACKEND = 1e-06
        EPS_NORM = 1e-05
        key = jax.random.key(seed)
        ks = jax.random.split(key, 8)
        q = jax.random.normal(ks[0], (B, S, E), jnp.float32)
        k = jax.random.normal(ks[1], (B, S, E), jnp.float32)
        v = jax.random.normal(ks[2], (B, S, E), jnp.float32)
        igate_w = jax.random.normal(ks[3], (NH, 3 * E), jnp.float32) * 0.02
        igate_b = jax.random.normal(ks[4], (NH,), jnp.float32) * 0.1
        fgate_w = jax.random.normal(ks[5], (NH, 3 * E), jnp.float32) * 0.02
        fgate_b = jnp.linspace(3.0, 6.0, NH).astype(jnp.float32)
        norm_w = 1.0 + 0.1 * jax.random.normal(ks[6], (E,), jnp.float32)
        return dict(q=q, k=k, v=v, igate_w=igate_w, igate_b=igate_b, fgate_w=fgate_w, fgate_b=fgate_b, norm_w=norm_w)
    _L2_xattn_all = _L2_xattn_setup()
    _L2_xattn_in = {k: v for k, v in _L2_xattn_all.items() if k in ('igate_w', 'igate_b', 'fgate_w', 'fgate_b', 'norm_w')}
    del _L2_xattn_all

    def _L2_ffn_setup():
        import jax, jax.numpy as jnp
        import numpy as np
        NUM_EXPERTS = 8
        TOP_K = 2
        D_MODEL = 128
        EXPERT_CAP = 64
        B, S = (4, 256)
        key = jax.random.key(seed)
        ks = jax.random.split(key, 4)
        scale = 1.0 / np.sqrt(D_MODEL)
        x = jax.random.normal(ks[0], (B, S, D_MODEL), dtype=jnp.float32)
        gate_w = jax.random.normal(ks[1], (D_MODEL, NUM_EXPERTS), dtype=jnp.float32) * scale
        w1 = jax.random.normal(ks[2], (NUM_EXPERTS, D_MODEL, EXPERT_CAP), dtype=jnp.float32) * scale
        b1 = jnp.zeros((NUM_EXPERTS, EXPERT_CAP), dtype=jnp.float32)
        w2 = jax.random.normal(ks[3], (NUM_EXPERTS, EXPERT_CAP, D_MODEL), dtype=jnp.float32) * (1.0 / np.sqrt(EXPERT_CAP))
        b2 = jnp.zeros((NUM_EXPERTS, D_MODEL), dtype=jnp.float32)
        return {'x': x, 'gate_w': gate_w, 'w1': w1, 'b1': b1, 'w2': w2, 'b2': b2}
    _L2_ffn_all = _L2_ffn_setup()
    _L2_ffn_in = {k: v for k, v in _L2_ffn_all.items() if k in ('gate_w', 'w1', 'b1', 'w2', 'b2')}
    del _L2_ffn_all

    def _L3_attn_setup():
        import jax, jax.numpy as jnp
        import numpy as np
        LORA_RANK = 16
        LORA_ALPHA = 32
        CHUNK_SIZE = 32
        TTT_LR = 0.01
        CLIP_THRESHOLD = 1.0
        SCALING = LORA_ALPHA / LORA_RANK
        LN_EPS = 1e-05

        def _forward(x, Wb, init_A, init_B, ln_gamma, ln_beta, Wp):
            B_sz, Seq, k_dim = x.shape
            h_dim = Wb.shape[0]
            r = init_A.shape[1]
            nc = Seq // CHUNK_SIZE
            base_out = x @ Wb.T
            xd = jax.lax.stop_gradient(x)
            mu = jnp.mean(xd, axis=-1, keepdims=True)
            var = jnp.mean((xd - mu) ** 2, axis=-1, keepdims=True)
            xn = (xd - mu) * jax.lax.rsqrt(var + LN_EPS) * ln_gamma + ln_beta
            shifted = jnp.pad(xn[:, 1:, :], ((0, 0), (0, 1), (0, 0)))
            shifted = jax.lax.stop_gradient(shifted)
            V = shifted @ Wp.T
            Z = x.reshape(B_sz * nc, CHUNK_SIZE, k_dim)
            Vc = V.reshape(B_sz * nc, CHUNK_SIZE, h_dim)
            proj_in = Z @ init_B.T
            dA = jnp.einsum('bch,bcr->bhr', Vc, proj_in)
            proj_err = Vc @ init_A
            dB = jnp.einsum('bcr,bck->brk', proj_err, Z)
            dA = dA.reshape(B_sz, nc, h_dim, r)
            dB = dB.reshape(B_sz, nc, r, k_dim)
            accA = jnp.cumsum(dA, axis=1)
            accB = jnp.cumsum(dB, axis=1)
            accA = jnp.concatenate([jnp.zeros_like(accA[:, :1]), accA[:, :-1]], axis=1)
            accB = jnp.concatenate([jnp.zeros_like(accB[:, :1]), accB[:, :-1]], axis=1)
            lr = TTT_LR * SCALING
            rawA = (lr * accA).reshape(-1, h_dim, r)
            rawB = (lr * accB).reshape(-1, r, k_dim)
            norm_sq = jnp.sum(rawA.astype(jnp.float32) ** 2, axis=(-2, -1), keepdims=True) + jnp.sum(rawB.astype(jnp.float32) ** 2, axis=(-2, -1), keepdims=True)
            total_norm = jnp.sqrt(norm_sq)
            coef = jnp.minimum(CLIP_THRESHOLD / (total_norm + 1e-06), 1.0).astype(rawA.dtype)
            A_eff = init_A[None] - rawA * coef
            B_eff = init_B[None] - rawB * coef
            mid = jnp.einsum('bck,brk->bcr', Z, B_eff)
            lora = jnp.einsum('bcr,bhr->bch', mid, A_eff)
            lora = lora.reshape(B_sz, Seq, h_dim)
            return base_out + lora * SCALING
        key = jax.random.key(seed)
        ks = jax.random.split(key, 5)
        B, S, K, H = (2, 1024, 128, 128)
        x = jax.random.normal(ks[0], (B, S, K), dtype=jnp.float32)
        Wb = jax.random.normal(ks[1], (H, K), dtype=jnp.float32) / np.sqrt(K)
        init_A = jax.random.normal(ks[2], (H, LORA_RANK), dtype=jnp.float32) * 0.01
        init_B = jax.random.normal(ks[3], (LORA_RANK, K), dtype=jnp.float32) * 0.01
        ln_gamma = jnp.ones((K,), dtype=jnp.float32)
        ln_beta = jnp.zeros((K,), dtype=jnp.float32)
        Wp = jax.random.normal(ks[4], (H, K), dtype=jnp.float32) / np.sqrt(K)
        return {'x': x, 'Wb': Wb, 'init_A': init_A, 'init_B': init_B, 'ln_gamma': ln_gamma, 'ln_beta': ln_beta, 'Wp': Wp}
    _L3_attn_all = _L3_attn_setup()
    _L3_attn_in = {k: v for k, v in _L3_attn_all.items() if k in ('Wb', 'init_A', 'init_B', 'ln_gamma', 'ln_beta', 'Wp')}
    del _L3_attn_all

    def _L3_xattn_setup():
        import jax, jax.numpy as jnp
        import numpy as np
        B, SQ, SK, D, H = (2, 256, 512, 128, 16)
        HD = D // H

        def _local_allowed_mask(num_q, num_k):
            kpq, extra = (num_k // num_q, num_k % num_q)
            i = jnp.arange(num_q)
            start = i * kpq + jnp.minimum(i, extra)
            end = start + kpq + (i < extra)
            j = jnp.arange(num_k)
            return (j[None, :] >= start[:, None]) & (j[None, :] < end[:, None])
        key = jax.random.key(seed)
        ks = jax.random.split(key, 6)
        s = 0.02
        return {'x': jax.random.normal(ks[0], (B, SQ, D), jnp.float32), 'c': jax.random.normal(ks[1], (B, SK, D), jnp.float32), 'Wq': jax.random.normal(ks[2], (D, D), jnp.float32) * s, 'bq': jnp.zeros((D,), jnp.float32), 'Wk': jax.random.normal(ks[3], (D, D), jnp.float32) * s, 'bk': jnp.zeros((D,), jnp.float32), 'Wv': jax.random.normal(ks[4], (D, D), jnp.float32) * s, 'bv': jnp.zeros((D,), jnp.float32), 'Wo': jax.random.normal(ks[5], (D, D), jnp.float32) * s, 'bo': jnp.zeros((D,), jnp.float32)}
    _L3_xattn_all = _L3_xattn_setup()
    _L3_xattn_in = {k: v for k, v in _L3_xattn_all.items() if k in ('Wq', 'bq', 'Wk', 'bk', 'Wv', 'bv', 'Wo', 'bo')}
    del _L3_xattn_all

    def _L3_ffn_setup():
        import jax, jax.numpy as jnp
        import numpy as np
        B, S, D, F, O = (4, 256, 128, 512, 128)
        E, NS, K = (4, 2, 2)
        key = jax.random.key(seed)
        ks = jax.random.split(key, 6)

        def w(k, shape, fan_in):
            return jax.random.normal(k, shape, jnp.float32) * fan_in ** (-0.5)
        return {'x': jax.random.normal(ks[0], (B, S, D), jnp.float32), 'gate_w': w(ks[1], (D, E), D), 'gate_b': jnp.zeros((E,), jnp.float32), 'sw1': w(ks[2], (NS, D, F), D), 'sb1': jnp.zeros((NS, F), jnp.float32), 'sw2': w(ks[3], (NS, F, O), F), 'sb2': jnp.zeros((NS, O), jnp.float32), 'rw1': w(ks[4], (E, D, F), D), 'rb1': jnp.zeros((E, F), jnp.float32), 'rw2': w(ks[5], (E, F, O), F), 'rb2': jnp.zeros((E, O), jnp.float32)}
    _L3_ffn_all = _L3_ffn_setup()
    _L3_ffn_in = {k: v for k, v in _L3_ffn_all.items() if k in ('gate_w', 'gate_b', 'sw1', 'sb1', 'sw2', 'sb2', 'rw1', 'rb1', 'rw2', 'rb2')}
    del _L3_ffn_all
    return {'x': x, 'ctx_1024': ctx_1024, 'L0_attn_bv_q': _L0_attn_in['bv_q'], 'L0_attn_bv_k': _L0_attn_in['bv_k'], 'L0_attn_bv_v': _L0_attn_in['bv_v'], 'L0_xattn_Wq': _L0_xattn_in['Wq'], 'L0_xattn_Wk': _L0_xattn_in['Wk'], 'L0_xattn_Wv': _L0_xattn_in['Wv'], 'L0_xattn_Wo': _L0_xattn_in['Wo'], 'L0_xattn_ln_gamma': _L0_xattn_in['ln_gamma'], 'L0_xattn_ln_beta': _L0_xattn_in['ln_beta'], 'L0_ffn_Wr1': _L0_ffn_in['Wr1'], 'L0_ffn_br1': _L0_ffn_in['br1'], 'L0_ffn_Wr2': _L0_ffn_in['Wr2'], 'L0_ffn_br2': _L0_ffn_in['br2'], 'L0_ffn_Ws1': _L0_ffn_in['Ws1'], 'L0_ffn_bs1': _L0_ffn_in['bs1'], 'L0_ffn_Ws2': _L0_ffn_in['Ws2'], 'L0_ffn_bs2': _L0_ffn_in['bs2'], 'L0_ffn_We1': _L0_ffn_in['We1'], 'L0_ffn_be1': _L0_ffn_in['be1'], 'L0_ffn_We2': _L0_ffn_in['We2'], 'L0_ffn_be2': _L0_ffn_in['be2'], 'L1_attn_w_qkv': _L1_attn_in['w_qkv'], 'L1_attn_b_qkv': _L1_attn_in['b_qkv'], 'L1_attn_w_g1': _L1_attn_in['w_g1'], 'L1_attn_b_g1': _L1_attn_in['b_g1'], 'L1_attn_w_g2': _L1_attn_in['w_g2'], 'L1_attn_b_g2': _L1_attn_in['b_g2'], 'L1_attn_w_out': _L1_attn_in['w_out'], 'L1_attn_b_out': _L1_attn_in['b_out'], 'L1_attn_ln_g': _L1_attn_in['ln_g'], 'L1_attn_ln_b': _L1_attn_in['ln_b'], 'L1_xattn_Wq': _L1_xattn_in['Wq'], 'L1_xattn_Wkv': _L1_xattn_in['Wkv'], 'L1_ffn_Wq': _L1_ffn_in['Wq'], 'L1_ffn_routers': _L1_ffn_in['routers'], 'L1_ffn_leaf_keys': _L1_ffn_in['leaf_keys'], 'L1_ffn_leaf_values': _L1_ffn_in['leaf_values'], 'L1_ffn_Wout_w': _L1_ffn_in['Wout_w'], 'L1_ffn_Wout_b': _L1_ffn_in['Wout_b'], 'L2_attn_Wq': _L2_attn_in['Wq'], 'L2_attn_Wk': _L2_attn_in['Wk'], 'L2_attn_Wv': _L2_attn_in['Wv'], 'L2_attn_Wo': _L2_attn_in['Wo'], 'L2_attn_bo': _L2_attn_in['bo'], 'L2_xattn_igate_w': _L2_xattn_in['igate_w'], 'L2_xattn_igate_b': _L2_xattn_in['igate_b'], 'L2_xattn_fgate_w': _L2_xattn_in['fgate_w'], 'L2_xattn_fgate_b': _L2_xattn_in['fgate_b'], 'L2_xattn_norm_w': _L2_xattn_in['norm_w'], 'L2_ffn_gate_w': _L2_ffn_in['gate_w'], 'L2_ffn_w1': _L2_ffn_in['w1'], 'L2_ffn_b1': _L2_ffn_in['b1'], 'L2_ffn_w2': _L2_ffn_in['w2'], 'L2_ffn_b2': _L2_ffn_in['b2'], 'L3_attn_Wb': _L3_attn_in['Wb'], 'L3_attn_init_A': _L3_attn_in['init_A'], 'L3_attn_init_B': _L3_attn_in['init_B'], 'L3_attn_ln_gamma': _L3_attn_in['ln_gamma'], 'L3_attn_ln_beta': _L3_attn_in['ln_beta'], 'L3_attn_Wp': _L3_attn_in['Wp'], 'L3_xattn_Wq': _L3_xattn_in['Wq'], 'L3_xattn_bq': _L3_xattn_in['bq'], 'L3_xattn_Wk': _L3_xattn_in['Wk'], 'L3_xattn_bk': _L3_xattn_in['bk'], 'L3_xattn_Wv': _L3_xattn_in['Wv'], 'L3_xattn_bv': _L3_xattn_in['bv'], 'L3_xattn_Wo': _L3_xattn_in['Wo'], 'L3_xattn_bo': _L3_xattn_in['bo'], 'L3_ffn_gate_w': _L3_ffn_in['gate_w'], 'L3_ffn_gate_b': _L3_ffn_in['gate_b'], 'L3_ffn_sw1': _L3_ffn_in['sw1'], 'L3_ffn_sb1': _L3_ffn_in['sb1'], 'L3_ffn_sw2': _L3_ffn_in['sw2'], 'L3_ffn_sb2': _L3_ffn_in['sb2'], 'L3_ffn_rw1': _L3_ffn_in['rw1'], 'L3_ffn_rb1': _L3_ffn_in['rb1'], 'L3_ffn_rw2': _L3_ffn_in['rw2'], 'L3_ffn_rb2': _L3_ffn_in['rb2']}

def reference(x, ctx_1024, L0_attn_bv_q, L0_attn_bv_k, L0_attn_bv_v, L0_xattn_Wq, L0_xattn_Wk, L0_xattn_Wv, L0_xattn_Wo, L0_xattn_ln_gamma, L0_xattn_ln_beta, L0_ffn_Wr1, L0_ffn_br1, L0_ffn_Wr2, L0_ffn_br2, L0_ffn_Ws1, L0_ffn_bs1, L0_ffn_Ws2, L0_ffn_bs2, L0_ffn_We1, L0_ffn_be1, L0_ffn_We2, L0_ffn_be2, L1_attn_w_qkv, L1_attn_b_qkv, L1_attn_w_g1, L1_attn_b_g1, L1_attn_w_g2, L1_attn_b_g2, L1_attn_w_out, L1_attn_b_out, L1_attn_ln_g, L1_attn_ln_b, L1_xattn_Wq, L1_xattn_Wkv, L1_ffn_Wq, L1_ffn_routers, L1_ffn_leaf_keys, L1_ffn_leaf_values, L1_ffn_Wout_w, L1_ffn_Wout_b, L2_attn_Wq, L2_attn_Wk, L2_attn_Wv, L2_attn_Wo, L2_attn_bo, L2_xattn_igate_w, L2_xattn_igate_b, L2_xattn_fgate_w, L2_xattn_fgate_b, L2_xattn_norm_w, L2_ffn_gate_w, L2_ffn_w1, L2_ffn_b1, L2_ffn_w2, L2_ffn_b2, L3_attn_Wb, L3_attn_init_A, L3_attn_init_B, L3_attn_ln_gamma, L3_attn_ln_beta, L3_attn_Wp, L3_xattn_Wq, L3_xattn_bq, L3_xattn_Wk, L3_xattn_bk, L3_xattn_Wv, L3_xattn_bv, L3_xattn_Wo, L3_xattn_bo, L3_ffn_gate_w, L3_ffn_gate_b, L3_ffn_sw1, L3_ffn_sb1, L3_ffn_sw2, L3_ffn_sb2, L3_ffn_rw1, L3_ffn_rb1, L3_ffn_rw2, L3_ffn_rb2):
    import jax
    import jax.numpy as jnp

    def _L0_attn_ref(x, bv_q, bv_k, bv_v):
        import jax, jax.numpy as jnp
        import numpy as np
        B, T, D = (4, 256, 128)

        def ste_sign(x):
            return jax.lax.stop_gradient(jnp.sign(x) - x) + x
        d = x.shape[-1]
        scale = d ** (-0.5)
        bq = ste_sign(bv_q)
        bk = ste_sign(bv_k)
        bv = ste_sign(bv_v)
        Q = ste_sign(x * bq)
        K = ste_sign(x * bk)
        V = x * bv
        scores = jnp.einsum('btd,bsd->bts', Q, K) * scale
        t = x.shape[1]
        causal = jnp.tril(jnp.ones((t, t), dtype=bool))
        scores = jnp.where(causal, scores, -jnp.inf)
        attn = jax.nn.sigmoid(scores * 4.0)
        attn = jnp.where(causal, attn, 0.0)
        return jnp.einsum('bts,bsd->btd', attn, V)

    def _L0_xattn_ref(query, key, value, Wq, Wk, Wv, Wo, ln_gamma, ln_beta):
        import jax, jax.numpy as jnp
        import numpy as np
        D_MODEL = 128
        NUM_HEADS = 16
        D_K = D_MODEL // NUM_HEADS
        LN_EPS = 1e-05

        def _layernorm(x, gamma, beta):
            mu = jnp.mean(x, axis=-1, keepdims=True)
            var = jnp.var(x, axis=-1, keepdims=True)
            return (x - mu) * jax.lax.rsqrt(var + LN_EPS) * gamma + beta
        B, S, _ = query.shape
        Q = query @ Wq.T
        K = key @ Wk.T
        V = value @ Wv.T
        Q = _layernorm(Q, ln_gamma, ln_beta)
        K = _layernorm(K, ln_gamma, ln_beta)
        Q = Q.reshape(B, S, NUM_HEADS, D_K).transpose(0, 2, 1, 3)
        K = K.reshape(B, S, NUM_HEADS, D_K).transpose(0, 2, 1, 3)
        V = V.reshape(B, S, NUM_HEADS, D_K).transpose(0, 2, 1, 3)
        scores = jnp.einsum('bhqd,bhkd->bhqk', Q, K) / np.sqrt(D_K).astype(np.float32)
        attn = jax.nn.softmax(scores, axis=-1)
        context = jnp.einsum('bhqk,bhkd->bhqd', attn, V)
        context = context.transpose(0, 2, 1, 3).reshape(B, S, D_MODEL)
        return context @ Wo.T

    def _L0_ffn_ref(x, Wr1, br1, Wr2, br2, Ws1, bs1, Ws2, bs2, We1, be1, We2, be2):
        import jax, jax.numpy as jnp
        import numpy as np
        B, T, C = (2, 64, 128)
        I = 512
        E = 8
        K = 2
        Bb, Tt, Cc = x.shape
        xf = x.reshape(-1, Cc)
        logits = jax.nn.relu(xf @ Wr1 + br1) @ Wr2 + br2
        gates = jax.nn.softmax(logits, axis=-1)
        tg, ti = jax.lax.top_k(gates, K)
        tg = jax.nn.softmax(tg / K, axis=-1)
        out = jax.nn.silu(xf @ Ws1 + bs1) @ Ws2 + bs2
        for e in range(E):
            h = jax.nn.silu(xf @ We1[e] + be1[e]) @ We2[e] + be2[e]
            w = jnp.sum(tg * (ti == e), axis=-1)
            out = out + w[:, None] * h
        return out.reshape(Bb, Tt, Cc)

    def _L1_attn_ref(x, w_qkv, b_qkv, w_g1, b_g1, w_g2, b_g2, w_out, b_out, ln_g, ln_b):
        import jax, jax.numpy as jnp
        import numpy as np
        B, N, H = (4, 512, 128)
        NUM_HEADS = 16
        HEAD_DIM = H // NUM_HEADS
        EPS = 1e-05

        def _layernorm(x, g, b):
            mu = jnp.mean(x, axis=-1, keepdims=True)
            var = jnp.mean(jnp.square(x - mu), axis=-1, keepdims=True)
            return (x - mu) * jax.lax.rsqrt(var + EPS) * g + b
        b, n, hdim = x.shape
        qkv = jnp.einsum('bnh,oh->bno', x, w_qkv) + b_qkv
        q, k, v = jnp.split(qkv, 3, axis=-1)

        def split_heads(t):
            return t.reshape(b, n, NUM_HEADS, HEAD_DIM).transpose(0, 2, 1, 3)
        q, k, v = (split_heads(q), split_heads(k), split_heads(v))
        q = jax.nn.silu(q)
        k = jax.nn.softmax(k, axis=-2)
        if n <= HEAD_DIM:
            attn = jnp.einsum('bhnd,bhmd->bhnm', q, k)
            out = jnp.einsum('bhnm,bhmd->bhnd', attn, v)
        else:
            kv = jnp.einsum('bhnd,bhne->bhde', k, v)
            out = jnp.einsum('bhnd,bhde->bhne', q, kv)
        out = out.transpose(0, 2, 1, 3).reshape(b, n, hdim)
        out = _layernorm(out, ln_g, ln_b)
        gate_hidden = jnp.einsum('bnh,dh->bnd', x, w_g1) + b_g1
        gate = jax.nn.sigmoid(jnp.einsum('bnd,hd->bnh', gate_hidden, w_g2) + b_g2)
        out = out * gate
        out = jnp.einsum('bnh,oh->bno', out, w_out) + b_out
        return out

    def _L1_xattn_ref(hidden_states, decoder_hidden_states, Wq, Wkv):
        import jax, jax.numpy as jnp
        import numpy as np
        EMBED_DIM = 128
        B, QL, KL = (4, 256, 256)
        d = Wq.shape[0]
        scale = 1.0 / np.sqrt(d)
        query = hidden_states @ Wq
        kv = decoder_hidden_states @ Wkv
        key, value = jnp.split(kv, 2, axis=-1)
        scores = jnp.einsum('bqd,bkd->bqk', query, key) * scale
        w = jax.nn.softmax(scores, axis=-1)
        return jnp.einsum('bqk,bkd->bqd', w, value)

    def _L1_ffn_ref(x, Wq, routers, leaf_keys, leaf_values, Wout_w, Wout_b):
        import jax, jax.numpy as jnp
        import numpy as np
        D_MODEL = 128
        DEPTH = 8
        M = 2 ** DEPTH
        N_INTERNAL = M - 1
        B, T = (8, 512)

        def _leaf_probs(gate):
            BT = gate.shape[0]
            lp = jnp.ones((BT, M), dtype=gate.dtype)
            for level in range(DEPTH):
                n = 2 ** level
                half = M // (2 * n)
                g = gate[:, n - 1:2 * n - 1]
                f = jnp.stack([1.0 - g, g], axis=-1)
                f = jnp.broadcast_to(f[..., None], (BT, n, 2, half))
                lp = lp * f.reshape(BT, M)
            return lp
        Bv, Tv, d = x.shape
        q = jnp.einsum('btd,ed->bte', x, Wq)
        q_flat = q.reshape(Bv * Tv, d)
        gate = jax.nn.sigmoid(q_flat @ routers.T)
        leaf_prob = _leaf_probs(gate)
        ret = (leaf_prob @ leaf_values).reshape(Bv, Tv, d)
        return jnp.einsum('btd,ed->bte', ret, Wout_w) + Wout_b

    def _L2_attn_ref(x, Wq, Wk, Wv, Wo, bo):
        import jax, jax.numpy as jnp
        import numpy as np
        B, N, QD = (4, 512, 128)
        HEADS, DIM_HEAD = (8, 64)
        HID = HEADS * DIM_HEAD
        SCALE = DIM_HEAD ** (-0.5)
        b, n, _ = x.shape
        q = x @ Wq
        k = x @ Wk
        v = x @ Wv

        def split_heads(t):
            return t.reshape(b, n, HEADS, DIM_HEAD).transpose(0, 2, 3, 1)
        q = split_heads(q)
        k = split_heads(k)
        v = split_heads(v)
        q = jax.nn.softmax(q, axis=-2) * SCALE
        k = jax.nn.softmax(k, axis=-1)
        context = jnp.einsum('bhdn,bhen->bhde', k, v)
        out = jnp.einsum('bhde,bhdn->bhen', context, q)
        out = out.transpose(0, 3, 1, 2).reshape(b, n, HID)
        return out @ Wo + bo

    def _L2_xattn_ref(q, k, v, igate_w, igate_b, fgate_w, fgate_b, norm_w):
        import jax, jax.numpy as jnp
        import numpy as np
        B, S, E, NH = (1, 256, 128, 8)
        DH = E // NH
        EPS_BACKEND = 1e-06
        EPS_NORM = 1e-05
        Bq, Sq, Eq = q.shape
        nh = igate_w.shape[0]
        dh = Eq // nh
        gate_in = jnp.concatenate([q, k, v], axis=-1)
        ig = jnp.transpose(gate_in @ igate_w.T + igate_b, (0, 2, 1))
        fg = jnp.transpose(gate_in @ fgate_w.T + fgate_b, (0, 2, 1))
        qh = q.reshape(Bq, Sq, nh, dh).transpose(0, 2, 1, 3)
        kh = k.reshape(Bq, Sq, nh, dh).transpose(0, 2, 1, 3)
        vh = v.reshape(Bq, Sq, nh, dh).transpose(0, 2, 1, 3)
        log_f_cum = jnp.cumsum(jax.nn.log_sigmoid(fg), axis=-1)
        log_fg_mat = log_f_cum[:, :, :, None] - log_f_cum[:, :, None, :]
        ltr = jnp.tril(jnp.ones((Sq, Sq), dtype=bool))
        log_D = jnp.where(ltr, log_fg_mat + ig[:, :, None, :], -jnp.inf)
        max_log_D = jnp.max(log_D, axis=-1, keepdims=True)
        D = jnp.exp(log_D - max_log_D)
        qk = jnp.einsum('bhsd,bhtd->bhst', qh, kh) / jnp.sqrt(jnp.float32(dh))
        C = qk * D
        normalizer = jnp.maximum(jnp.abs(jnp.sum(C, axis=-1, keepdims=True)), jnp.exp(-max_log_D))
        h = jnp.einsum('bhst,bhtd->bhsd', C / (normalizer + EPS_BACKEND), vh)
        mean = jnp.mean(h, axis=-1, keepdims=True)
        var = jnp.var(h, axis=-1, keepdims=True)
        h_norm = (h - mean) / jnp.sqrt(var + EPS_NORM)
        h_norm = h_norm * norm_w.reshape(nh, dh)[None, :, None, :]
        return h_norm.transpose(0, 2, 1, 3).reshape(Bq, Sq, Eq)

    def _L2_ffn_ref(x, gate_w, w1, b1, w2, b2):
        import jax, jax.numpy as jnp
        import numpy as np
        NUM_EXPERTS = 8
        TOP_K = 2
        D_MODEL = 128
        EXPERT_CAP = 64
        B, S = (4, 256)
        Bx, Sx, D = x.shape
        xt = x.reshape(-1, D)
        gates = jax.nn.softmax(xt @ gate_w, axis=-1)
        topk_g, topk_i = jax.lax.top_k(gates, TOP_K)
        tok_w = topk_g.sum(axis=-1)
        sel = (topk_i[:, :, None] == jnp.arange(NUM_EXPERTS)[None, None, :]).any(axis=1)
        h = jax.nn.gelu(jnp.einsum('nd,edh->enh', xt, w1) + b1[:, None, :], approximate=False)
        y = jnp.einsum('enh,ehd->end', h, w2) + b2[:, None, :]
        out = jnp.einsum('end,ne,n->nd', y, sel.astype(x.dtype), tok_w)
        return out.reshape(Bx, Sx, D)

    def _L3_attn_ref(x, Wb, init_A, init_B, ln_gamma, ln_beta, Wp):
        import jax, jax.numpy as jnp
        import numpy as np
        LORA_RANK = 16
        LORA_ALPHA = 32
        CHUNK_SIZE = 32
        TTT_LR = 0.01
        CLIP_THRESHOLD = 1.0
        SCALING = LORA_ALPHA / LORA_RANK
        LN_EPS = 1e-05

        def _forward(x, Wb, init_A, init_B, ln_gamma, ln_beta, Wp):
            B_sz, Seq, k_dim = x.shape
            h_dim = Wb.shape[0]
            r = init_A.shape[1]
            nc = Seq // CHUNK_SIZE
            base_out = x @ Wb.T
            xd = jax.lax.stop_gradient(x)
            mu = jnp.mean(xd, axis=-1, keepdims=True)
            var = jnp.mean((xd - mu) ** 2, axis=-1, keepdims=True)
            xn = (xd - mu) * jax.lax.rsqrt(var + LN_EPS) * ln_gamma + ln_beta
            shifted = jnp.pad(xn[:, 1:, :], ((0, 0), (0, 1), (0, 0)))
            shifted = jax.lax.stop_gradient(shifted)
            V = shifted @ Wp.T
            Z = x.reshape(B_sz * nc, CHUNK_SIZE, k_dim)
            Vc = V.reshape(B_sz * nc, CHUNK_SIZE, h_dim)
            proj_in = Z @ init_B.T
            dA = jnp.einsum('bch,bcr->bhr', Vc, proj_in)
            proj_err = Vc @ init_A
            dB = jnp.einsum('bcr,bck->brk', proj_err, Z)
            dA = dA.reshape(B_sz, nc, h_dim, r)
            dB = dB.reshape(B_sz, nc, r, k_dim)
            accA = jnp.cumsum(dA, axis=1)
            accB = jnp.cumsum(dB, axis=1)
            accA = jnp.concatenate([jnp.zeros_like(accA[:, :1]), accA[:, :-1]], axis=1)
            accB = jnp.concatenate([jnp.zeros_like(accB[:, :1]), accB[:, :-1]], axis=1)
            lr = TTT_LR * SCALING
            rawA = (lr * accA).reshape(-1, h_dim, r)
            rawB = (lr * accB).reshape(-1, r, k_dim)
            norm_sq = jnp.sum(rawA.astype(jnp.float32) ** 2, axis=(-2, -1), keepdims=True) + jnp.sum(rawB.astype(jnp.float32) ** 2, axis=(-2, -1), keepdims=True)
            total_norm = jnp.sqrt(norm_sq)
            coef = jnp.minimum(CLIP_THRESHOLD / (total_norm + 1e-06), 1.0).astype(rawA.dtype)
            A_eff = init_A[None] - rawA * coef
            B_eff = init_B[None] - rawB * coef
            mid = jnp.einsum('bck,brk->bcr', Z, B_eff)
            lora = jnp.einsum('bcr,bhr->bch', mid, A_eff)
            lora = lora.reshape(B_sz, Seq, h_dim)
            return base_out + lora * SCALING
        return _forward(x, Wb, init_A, init_B, ln_gamma, ln_beta, Wp)

    def _L3_xattn_ref(x, c, Wq, bq, Wk, bk, Wv, bv, Wo, bo):
        import jax, jax.numpy as jnp
        import numpy as np
        B, SQ, SK, D, H = (2, 256, 512, 128, 16)
        HD = D // H

        def _local_allowed_mask(num_q, num_k):
            kpq, extra = (num_k // num_q, num_k % num_q)
            i = jnp.arange(num_q)
            start = i * kpq + jnp.minimum(i, extra)
            end = start + kpq + (i < extra)
            j = jnp.arange(num_k)
            return (j[None, :] >= start[:, None]) & (j[None, :] < end[:, None])
        b, sq, d = x.shape
        sk = c.shape[1]
        scale = 1.0 / jnp.sqrt(jnp.asarray(HD, x.dtype))
        q = (x @ Wq.T + bq).reshape(b, sq, H, HD).transpose(0, 2, 1, 3)
        k = (c @ Wk.T + bk).reshape(b, sk, H, HD).transpose(0, 2, 1, 3)
        v = (c @ Wv.T + bv).reshape(b, sk, H, HD).transpose(0, 2, 1, 3)
        scores = jnp.einsum('bhqd,bhkd->bhqk', q, k) * scale
        allowed = _local_allowed_mask(sq, sk)
        neg = jnp.asarray(jnp.finfo(scores.dtype).min, scores.dtype)
        scores = jnp.where(allowed[None, None], scores, neg)
        attn = jax.nn.softmax(scores, axis=-1)
        out = jnp.einsum('bhqk,bhkd->bhqd', attn, v)
        out = out.transpose(0, 2, 1, 3).reshape(b, sq, d)
        return out @ Wo.T + bo

    def _L3_ffn_ref(x, gate_w, gate_b, sw1, sb1, sw2, sb2, rw1, rb1, rw2, rb2):
        import jax, jax.numpy as jnp
        import numpy as np
        B, S, D, F, O = (4, 256, 128, 512, 128)
        E, NS, K = (4, 2, 2)
        weights = jax.nn.softmax(x @ gate_w + gate_b, axis=-1)
        topk_w, topk_i = jax.lax.top_k(weights, K)
        sh = jax.nn.relu(jnp.einsum('bsd,ndf->bsnf', x, sw1) + sb1)
        shared = (jnp.einsum('bsnf,nfo->bsno', sh, sw2) + sb2).sum(axis=2) / NS
        rh = jax.nn.relu(jnp.einsum('bsd,edf->bsef', x, rw1) + rb1)
        eo = jnp.einsum('bsef,efo->bseo', rh, rw2) + rb2
        gathered = jnp.take_along_axis(eo, topk_i[..., None], axis=2)
        routed = (gathered * topk_w[..., None]).sum(axis=2)
        return shared + routed
    x = x + _L0_attn_ref(_layernorm(x, axis=-1), L0_attn_bv_q, L0_attn_bv_k, L0_attn_bv_v)
    x = x + _L0_xattn_ref(_layernorm(x, axis=-1), ctx_1024, ctx_1024, L0_xattn_Wq, L0_xattn_Wk, L0_xattn_Wv, L0_xattn_Wo, L0_xattn_ln_gamma, L0_xattn_ln_beta)
    x = x + _L0_ffn_ref(_layernorm(x, axis=-1), L0_ffn_Wr1, L0_ffn_br1, L0_ffn_Wr2, L0_ffn_br2, L0_ffn_Ws1, L0_ffn_bs1, L0_ffn_Ws2, L0_ffn_bs2, L0_ffn_We1, L0_ffn_be1, L0_ffn_We2, L0_ffn_be2)
    x = x + _L1_attn_ref(_layernorm(x, axis=-1), L1_attn_w_qkv, L1_attn_b_qkv, L1_attn_w_g1, L1_attn_b_g1, L1_attn_w_g2, L1_attn_b_g2, L1_attn_w_out, L1_attn_b_out, L1_attn_ln_g, L1_attn_ln_b)
    x = x + _L1_xattn_ref(_layernorm(x, axis=-1), ctx_1024, L1_xattn_Wq, L1_xattn_Wkv)
    x = x + _L1_ffn_ref(_layernorm(x, axis=-1), L1_ffn_Wq, L1_ffn_routers, L1_ffn_leaf_keys, L1_ffn_leaf_values, L1_ffn_Wout_w, L1_ffn_Wout_b)
    x = x + _L2_attn_ref(_layernorm(x, axis=-1), L2_attn_Wq, L2_attn_Wk, L2_attn_Wv, L2_attn_Wo, L2_attn_bo)
    x = x + _L2_xattn_ref(_layernorm(x, axis=-1), ctx_1024, ctx_1024, L2_xattn_igate_w, L2_xattn_igate_b, L2_xattn_fgate_w, L2_xattn_fgate_b, L2_xattn_norm_w)
    x = x + _L2_ffn_ref(_layernorm(x, axis=-1), L2_ffn_gate_w, L2_ffn_w1, L2_ffn_b1, L2_ffn_w2, L2_ffn_b2)
    x = x + _L3_attn_ref(_layernorm(x, axis=-1), L3_attn_Wb, L3_attn_init_A, L3_attn_init_B, L3_attn_ln_gamma, L3_attn_ln_beta, L3_attn_Wp)
    x = x + _L3_xattn_ref(_layernorm(x, axis=-1), ctx_1024, L3_xattn_Wq, L3_xattn_bq, L3_xattn_Wk, L3_xattn_bk, L3_xattn_Wv, L3_xattn_bv, L3_xattn_Wo, L3_xattn_bo)
    x = x + _L3_ffn_ref(_layernorm(x, axis=-1), L3_ffn_gate_w, L3_ffn_gate_b, L3_ffn_sw1, L3_ffn_sb1, L3_ffn_sw2, L3_ffn_sb2, L3_ffn_rw1, L3_ffn_rb1, L3_ffn_rw2, L3_ffn_rb2)
    return x

_drawn_inputs = setup_inputs


def setup_inputs(seed=0):
    import zlib

    import numpy as np

    out = dict(_drawn_inputs(seed))
    spreads = {'L0_xattn_ln_gamma': (1.0, 0.2),
     'L0_xattn_ln_beta': (0.0, 0.685),
     'L0_ffn_br1': (0.0, 0.8),
     'L0_ffn_br2': (0.0, 0.1),
     'L0_ffn_bs1': (0.0, 0.602),
     'L0_ffn_bs2': (0.0, 0.1),
     'L0_ffn_be1': (0.0, 0.782),
     'L0_ffn_be2': (0.0, 0.285),
     'L1_attn_ln_g': (1.0, 0.6),
     'L1_attn_ln_b': (0.0, 0.8),
     'L2_ffn_b1': (0.0, 0.583),
     'L2_ffn_b2': (0.0, 0.399),
     'L3_attn_ln_gamma': (1.0, 0.6),
     'L3_attn_ln_beta': (0.0, 2.0),
     'L3_xattn_bq': (0.0, 0.1),
     'L3_xattn_bk': (0.0, 0.1),
     'L3_xattn_bv': (0.0, 0.8),
     'L3_xattn_bo': (0.0, 0.363),
     'L3_ffn_gate_b': (0.0, 0.661),
     'L3_ffn_sb1': (0.0, 0.789),
     'L3_ffn_sb2': (0.0, 0.536),
     'L3_ffn_rb1': (0.0, 0.8),
     'L3_ffn_rb2': (0.0, 0.611)}
    factors = {'L0_ffn_Wr1': 4.951,
     'L0_ffn_Wr2': 2.99,
     'L0_ffn_Ws1': 2.74,
     'L0_ffn_We1': 3.522,
     'L0_ffn_We2': 3.347,
     'L1_attn_b_qkv': 5.7,
     'L1_attn_w_g1': 8.0,
     'L1_attn_b_g1': 60.506,
     'L1_attn_w_g2': 8.0,
     'L1_attn_b_g2': 43.134,
     'L1_attn_b_out': 5.87,
     'L1_ffn_Wq': 8.0,
     'L1_ffn_routers': 8.0,
     'L1_ffn_leaf_values': 8.0,
     'L1_ffn_Wout_w': 8.0,
     'L1_ffn_Wout_b': 5.07,
     'L2_attn_Wq': 8.0,
     'L2_attn_Wk': 8.0,
     'L2_attn_Wv': 4.277,
     'L2_attn_Wo': 4.422,
     'L2_attn_bo': 4.105,
     'L2_xattn_igate_b': 64.0,
     'L2_xattn_fgate_w': 30.264,
     'L2_xattn_fgate_b': 10.714,
     'L3_attn_init_B': 9.32,
     'L3_xattn_Wv': 4.732,
     'L3_xattn_Wo': 4.452,
     'L3_attn_init_A': 3.389,
     'L3_attn_Wp': 2.673}
    for name, (base, spread) in spreads.items():
        noise = np.random.default_rng([zlib.crc32(name.encode()), seed]).standard_normal(out[name].shape)
        drawn = base * np.exp(spread * noise) if base else spread * noise
        out[name] = jnp.asarray(drawn.astype(out[name].dtype))
    for name, factor in factors.items():
        out[name] = (out[name] * factor).astype(out[name].dtype)
    return out
```

```python
import numpy as np
import concourse.bass as bass
from concourse import mybir
from contextlib import ExitStack

F32 = mybir.dt.float32
ACT = mybir.ActivationFunctionType
ALU = mybir.AluOpType
AX = mybir.AxisListType

P = 128
BATCHES, SEQ, D = 64, 64, 128
TOKENS = BATCHES * SEQ
SLOTS = 4
TILES = 2
SLOT_TOKENS = TILES * P
SLOT_BATCHES = SLOT_TOKENS // SEQ
GROUPS = TOKENS // (SLOTS * SLOT_TOKENS)
HALVES = P // SEQ
BANK = 512
EPS = 1e-5
CHUNK, RANK = 32, 16
TTT_LR, TTT_SCALING, TTT_CLIP = 0.01, 2.0, 1.0
CTXV = 8 * 17

SIGNALS = """
x_updated bias_added ln_stats ln_rstd ln_y pool_step ln_yT_psum ln_yT bin_z bin_sign bin_qk bin_sigmoid bin_masked
layer_out bin_scores projected mha_qk mha_qkT_psum mha_kheads mha_out mha_scores mha_exp mha_probsT_psum
mha_probsT mha_heads mha_outT_psum mha_outT mha_qkT mha_shifted inner_stats inner_rstd gate_shifted gate_exp
gate_logits gate_weights gate_wT_psum gate_wT moe_added moe_h moe_h2 moe_act moe_act2 moe_y moe_router
moe_relu gate_top gate_expw fst_h fst_gelu fst_wb fst_hw lin_kexp lin_silu lin_v lin_kt_psum lin_kt lin_kv
lin_kvm lin_gate lin_out lin_n lin_nT_psum lin_gated lin_kshift one_qk one_scores one_probs one_v
one_PT_psum one_PT one_max tree_q tree_logit tree_leaf tree_leafT_psum tree_leafT tree_ret tree_rT tree_gate
lha_kshift lha_q_psum lha_qshift lha_v_psum lha_kexp lha_v lha_kt_psum lha_qn lha_kt lha_qT_psum lha_qT
lha_oT lha_kv lha_kvm lha_oT_psum lha_qexp mls_arg mls_arg_psum mls_shift mls_qm mls_qk mls_C mls_out
mls_abs mls_sum mls_h mls_sq act_step mls_softplus mls_cum mls_em mls_D mls_var mls_rstd ttt_z ttt_zT_psum ttt_xnT ttt_p1 ttt_s1
ttt_p2 ttt_s2 ttt_d ttt_sq ttt_norm ttt_eff ttt_mid_psum ttt_mid ttt_nsq ttt_root ttt_squares ttt_raw dia_vT dve_step pe_step
""".split()


def nth(n, s):
    return n * SLOTS + s + 1


def spread(ap, axis, n):
    ap = ap.unsqueeze(axis)
    shape = list(ap.shape)
    shape[axis] = n
    return ap.broadcast_to(shape)


class Steps:

    def __init__(self, sem):
        self.sem, self.n = sem, 0

    def __call__(self, instruction):
        self.n += 1
        instruction.then_inc(self.sem, 1)
        return self.n


def constants():
    p, q = np.arange(P)[:, None], np.arange(P)[None, :]
    same = (p // SEQ) == (q // SEQ)
    f = np.float32
    s = np.arange(SEQ)[None, :]
    out = {
        "ident": (p == q).astype(f),
        "ones": np.ones((P, P), f),
        "causal": (same & (p <= q)).astype(f),
        "causal_neg": np.where(p % SEQ <= s, 0.0, -1e30).astype(f),
        "before8": np.tile((np.arange(8)[None, :] < np.arange(8)[:, None]).astype(f).reshape(1, 64), (P, 1)),
        "before4": np.tile((np.arange(4)[None, :] < np.arange(4)[:, None]).astype(f).reshape(1, 16), (P, 1)),
        "parity8": ((p // SEQ) == (q // 8) % 2).astype(f),
        "head_of_4": ((p % 32) // 8 == np.arange(4)[None, :]).astype(f),
        "head_of_2": ((p % 32) // 16 == np.arange(2)[None, :]).astype(f),
        "diag8": ((p // 8) == (q // 8)).astype(f),
        "diag64": same.astype(f),
        "rows_of_8": np.repeat((np.arange(8)[:, None] == np.arange(8)[None, :]).astype(f), SEQ, axis=1),
        "minus_delta8": -np.repeat((np.arange(8)[:, None] == np.arange(8)[None, :]).astype(f), SEQ, axis=1),
    }
    first = np.zeros((8, 1), f) + (np.arange(SLOT_TOKENS)[None, :] % SEQ == 0)
    out["not_first"] = (1.0 - first).astype(f)
    out["first_neg"] = np.where(first > 0, -3e38, 0.0).astype(f)
    r, t = np.arange(64)[:, None], np.arange(SLOT_TOKENS)[None, :]
    out["batch_rows"] = ((p // 32) == (np.arange(64)[None, :] // 16)).astype(f)
    out["batch_of_rank"] = ((r // 16) == np.arange(4)[None, :]).astype(f)
    out["second_chunk"] = np.where((r // 16 == t // SEQ) & (t % SEQ >= 32), TTT_SCALING, 0.0).astype(f)
    out["first_chunk"] = np.where(t % SEQ < 32, TTT_SCALING, 0.0).astype(f) + np.zeros((16, 1), f)
    return out


def columns(v):
    return v.reshape(-1, P).T


def chunked(w):
    return w.reshape(-1, P, w.shape[-1]).transpose(1, 0, 2).reshape(P, -1)


def rows(v):
    return np.broadcast_to(v.reshape(1, -1), (P, v.size))


def pieces(i):
    o = {}
    o["const"] = constants()
    o["bin"] = {"bq": i["L0_attn_bv_q"][:, None], "bk": i["L0_attn_bv_k"][:, None], "bv": rows(i["L0_attn_bv_v"])}
    o["mha"] = {"WqT": i["L0_xattn_Wq"].T, "WkT": i["L0_xattn_Wk"].T, "WvT": i["L0_xattn_Wv"].T,
                "WoT": i["L0_xattn_Wo"].T, "gamma": i["L0_xattn_ln_gamma"][:, None], "beta": i["L0_xattn_ln_beta"][:, None]}
    o["moe"] = {"Wr1": i["L0_ffn_Wr1"], "br1": i["L0_ffn_br1"][:, None], "Wr2": i["L0_ffn_Wr2"],
                "br2": i["L0_ffn_br2"][None, :],
                "b1": np.concatenate([columns(i["L0_ffn_bs1"])] + [columns(b) for b in i["L0_ffn_be1"]], axis=1),
                "b2": np.concatenate([i["L0_ffn_be2"], i["L0_ffn_bs2"][None, :]], axis=0),
                "W1_0": i["L0_ffn_Ws1"], "W2_0": chunked(i["L0_ffn_Ws2"])}
    for e in range(8):
        o["moe"][f"W1_{e + 1}"] = i["L0_ffn_We1"][e]
        o["moe"][f"W2_{e + 1}"] = chunked(i["L0_ffn_We2"][e])
    qkv, b = i["L1_attn_w_qkv"], i["L1_attn_b_qkv"]
    o["lin"] = {"WqT": qkv[0:P].T, "WkT": qkv[P:2 * P].T, "WvT": qkv[2 * P:3 * P].T,
                "bq": b[0:P][:, None], "bk": b[P:2 * P][:, None], "bv": rows(b[2 * P:3 * P]),
                "Wg1T": i["L1_attn_w_g1"].T, "bg1": i["L1_attn_b_g1"][:, None], "Wg2T": i["L1_attn_w_g2"].T,
                "bg2": i["L1_attn_b_g2"][:, None], "WoT": i["L1_attn_w_out"].T, "bo": rows(i["L1_attn_b_out"]),
                "gamma": i["L1_attn_ln_g"][:, None], "beta": i["L1_attn_ln_b"][:, None]}
    o["one"] = {"Wq": i["L1_xattn_Wq"], "Wk": i["L1_xattn_Wkv"][:, 0:P], "Wv": i["L1_xattn_Wkv"][:, P:2 * P]}
    routers = np.zeros((P, 256), np.float32)
    routers[:, 0:255] = i["L1_ffn_routers"].T
    o["tree"] = {"WqT": i["L1_ffn_Wq"].T, "routersT": routers, "leaves": chunked(i["L1_ffn_leaf_values"]),
                 "WoT": i["L1_ffn_Wout_w"].T, "bo": rows(i["L1_ffn_Wout_b"])}
    o["lha"] = {"Wq": i["L2_attn_Wq"], "Wk": i["L2_attn_Wk"], "Wv": i["L2_attn_Wv"],
                "Wo": chunked(i["L2_attn_Wo"]), "bo": rows(i["L2_attn_bo"])}
    o["mls"] = {"WfT": np.concatenate([i["L2_xattn_fgate_w"][:, j * P:(j + 1) * P].T for j in range(3)], axis=1),
                "WiT": np.concatenate([i["L2_xattn_igate_w"][:, j * P:(j + 1) * P].T for j in range(3)], axis=1),
                "bf": i["L2_xattn_fgate_b"][:, None], "bi": i["L2_xattn_igate_b"][:, None],
                "norm": rows(i["L2_xattn_norm_w"])}
    o["fst"] = {"gate": i["L2_ffn_gate_w"], "W1": i["L2_ffn_w1"].transpose(1, 0, 2).reshape(P, 512),
                "b1": columns(i["L2_ffn_b1"].reshape(-1)), "W2": chunked(i["L2_ffn_w2"].reshape(512, P)),
                "b2": i["L2_ffn_b2"]}
    o["ttt"] = {"WbT": i["L3_attn_Wb"].T, "A": i["L3_attn_init_A"], "AT": i["L3_attn_init_A"].T,
                "AT4": np.concatenate([i["L3_attn_init_A"].T] * SLOT_BATCHES, axis=0),
                "BT": i["L3_attn_init_B"].T, "gamma": i["L3_attn_ln_gamma"][:, None],
                "beta": i["L3_attn_ln_beta"][:, None], "WpT": i["L3_attn_Wp"].T}
    o["dia"] = {"WvT": i["L3_xattn_Wv"].T, "bv": i["L3_xattn_bv"][:, None], "WoT": i["L3_xattn_Wo"].T,
                "bo": rows(i["L3_xattn_bo"])}
    o["ffn"] = {"gate": i["L3_ffn_gate_w"], "gb": i["L3_ffn_gate_b"][None, :],
                "b1": np.concatenate([columns(b) for b in i["L3_ffn_sb1"]] + [columns(b) for b in i["L3_ffn_rb1"]], axis=1),
                "b2": np.concatenate([i["L3_ffn_rb2"], i["L3_ffn_sb2"]], axis=0)}
    for n in range(2):
        o["ffn"][f"W1_{n}"] = i["L3_ffn_sw1"][n]
        o["ffn"][f"W2_{n}"] = chunked(i["L3_ffn_sw2"][n])
    for e in range(4):
        o["ffn"][f"W1_{e + 2}"] = i["L3_ffn_rw1"][e]
        o["ffn"][f"W2_{e + 2}"] = chunked(i["L3_ffn_rw2"][e])
    return o


def pack(parts):
    width = sum(a.shape[1] for a in parts.values())
    out, where, at = np.zeros((P, width), np.float32), {}, 0
    for name, a in parts.items():
        out[0:a.shape[0], at:at + a.shape[1]] = a
        where[name] = (a.shape[0], at, a.shape[1])
        at += a.shape[1]
    return out, where


class Slot:

    def __init__(self, nc, ctx, s):
        def sb(name, shape):
            return ctx.enter_context(nc.sbuf_tensor(f"{name}{s}", shape, F32))
        self.x = sb("x", [P, TILES, D])
        self.y = sb("y", [P, TILES, D])
        self.yT = sb("yT", [P, SLOT_TOKENS])
        self.ctxT = sb("ctxT", [P, SLOT_TOKENS])
        self.ctxv = sb("ctxv", [P, TILES, CTXV])
        self.a = sb("a", [P, 1024])
        self.b = sb("b", [P, 1024])
        self.c = sb("c", [P, 1024])
        self.d = sb("d", [P, 1024])
        self.e = sb("e", [P, 1024])
        self.stats = sb("stats", [P, 4, 6])
        self.mv = sb("mv", [P, 4, 2])
        self.rstd = sb("rstd", [P, 16])
        self.t = sb("t", [P, 128])
        self.g = sb("g", [P, 48])
        self.wT = self.c[0:16, 768:1024]
        self.w = sb("w", [P, TILES, 9])
        self.w6 = sb("w6", [P, TILES, 6])
        self.ps = ctx.enter_context(nc.psum_tensor(f"ps{s}", [P, 2, BANK], F32))
        self.b0 = self.ps[:, 0, :]
        self.b1 = self.ps[:, 1, :]
        self.both = self.ps[:, :, :].rearrange("p b n -> p (b n)")


class Kern:
    pass


def tok(t):
    return slice(t * P, (t + 1) * P)


def bat(b):
    return slice(b * SEQ, (b + 1) * SEQ)


def half(b):
    return slice((b % HALVES) * SEQ, (b % HALVES + 1) * SEQ)


def statistics_dve(k, dve, L, s, sl):
    v, n = k.nc.vector, k.normalised_at.get(L)
    if n is None:
        return
    if L:
        dve.wait_ge(k.sem["x_updated"], nth(L - 1, s))
    for j in range(TILES):
        last = v.bn_stats(sl.stats[:, j, :], sl.x[:, j, :])
    now = k.step(last)
    dve.wait_ge(k.step.sem, now)
    for j in range(TILES):
        last = v.bn_aggr(sl.mv[:, j, :], sl.stats[:, j, :])
    last.then_inc(k.sem["ln_stats"], 1)


def normalise_dve(k, dve, L, n):
    sem, v = k.sem, k.nc.vector
    if L == 0:
        for s, sl in enumerate(k.slots):
            statistics_dve(k, dve, L, s, sl)
    for s, sl in enumerate(k.slots):
        dve.wait_ge(sem["ln_rstd"], nth(n, s))
        for j in range(TILES):
            last = v.tensor_scalar(sl.y[:, j, :], sl.x[:, j, :], sl.mv[:, j, 0:1], sl.rstd[:, j:j + 1],
                                   ALU.subtract, ALU.mult)
        last.then_inc(sem["ln_y"], 1)


def rstd_pool(k, pool, given, done, n, count):
    g = k.nc.gpsimd
    for s, sl in enumerate(k.slots):
        pool.wait_ge(k.sem[given], nth(n, s))
        last = g.tensor_scalar(sl.rstd[:, 0:count], sl.mv[:, 0:count, 1], EPS, None, ALU.add)
        now = k.pool_step(last)
        pool.wait_ge(k.pool_step.sem, now)
        g.tensor_tensor(sl.rstd[:, 0:count], sl.rstd[:, 0:count], k.minus_half[:, 0:count],
                        ALU.pow).then_inc(k.sem[done], 1)


def normalise_pe(k, pe, n):
    for s, sl in enumerate(k.slots):
        pe.wait_ge(k.sem["ln_y"], nth(n, s))
        for j in range(TILES):
            last = k.nc.tensor.transpose(sl.b0[:, tok(j)], sl.y[:, j, :], k.ident)
        last.then_inc(k.sem["ln_yT_psum"], 1)


def normalise_act(k, act, n):
    for s, sl in enumerate(k.slots):
        act.wait_ge(k.sem["ln_yT_psum"], nth(n, s))
        k.nc.scalar.copy(sl.yT[:, :], sl.b0[:, 0:SLOT_TOKENS]).then_inc(k.sem["ln_yT"], 1)


def bias_pool(k, pool, L, name):
    g, n = k.nc.gpsimd, k.normalised_at.get(L)
    for s, sl in enumerate(k.slots):
        if n is not None:
            pool.wait_ge(k.sem["ln_y"], nth(n, s))
        elif L:
            pool.wait_ge(k.sem["x_updated"], nth(L - 1, s))
        g.tensor_tensor(sl.x[:, :, :], sl.x[:, :, :], spread(k.w[name]["bo"], 1, TILES),
                        ALU.add).then_inc(k.sem["bias_added"], 1)


def add_to_x_dve(k, dve, L, ready, n, bank):
    for s, sl in enumerate(k.slots):
        dve.wait_ge(k.sem[ready], nth(n, s))
        if LAYERS[L] in BIASED:
            dve.wait_ge(k.sem["bias_added"], nth(BIASED.index(LAYERS[L]), s))
        out = (sl.b0, sl.b1)[bank][:, 0:SLOT_TOKENS].rearrange("p (t c) -> p t c", t=TILES)
        k.nc.vector.tensor_tensor(sl.x[:, :, :], sl.x[:, :, :], out, ALU.add).then_inc(k.sem["x_updated"], 1)
        statistics_dve(k, dve, L + 1, s, sl)


BIN_SCALE = 4.0 * D ** -0.5


def bin_dve(k, dve, L, n):
    sem, v, w = k.sem, k.nc.vector, k.w["bin"]
    for s, sl in enumerate(k.slots):
        z, val = sl.a[:, 0:512], sl.b[:, 0:256].rearrange("p (t c) -> p t c", t=TILES)
        dve.wait_ge(sem["ln_yT"], nth(n, s))
        v.tensor_scalar(z[:, 0:256], sl.yT[:, :], w["bq"], None, ALU.mult)
        v.tensor_scalar(z[:, 256:512], sl.yT[:, :], w["bk"], None, ALU.mult)
        v.tensor_tensor(val, sl.y[:, :, :], spread(w["bv"], 1, TILES), ALU.mult).then_inc(sem["bin_z"], 1)
    t = []
    for s, sl in enumerate(k.slots):
        dve.wait_ge(sem["bin_sign"], nth(0, s))
        t.append(k.step(v.tensor_tensor(sl.c[:, 0:512], sl.c[:, 0:512], sl.a[:, 0:512], ALU.subtract)))
        dve.wait_ge(k.step.sem, t[s])
        v.tensor_tensor(sl.d[:, 0:512], sl.c[:, 0:512], sl.a[:, 0:512], ALU.add).then_inc(sem["bin_qk"], 1)
    for s, sl in enumerate(k.slots):
        att = sl.e[:, 0:256].rearrange("p (t c) -> p t c", t=TILES)
        dve.wait_ge(sem["bin_sigmoid"], nth(0, s))
        v.tensor_tensor(att, att, spread(k.const["causal"], 1, TILES), ALU.mult).then_inc(sem["bin_masked"], 1)
    add_to_x_dve(k, dve, L, "layer_out", k.out_at["bin"], 1)


def bin_act(k, act):
    sem, a = k.sem, k.nc.scalar
    for s, sl in enumerate(k.slots):
        act.wait_ge(sem["bin_z"], nth(0, s))
        a.activation(sl.c[:, 0:512], sl.a[:, 0:512], ACT.Sign).then_inc(sem["bin_sign"], 1)
    for s, sl in enumerate(k.slots):
        act.wait_ge(sem["bin_scores"], nth(0, s))
        a.activation(sl.e[:, 0:256], sl.b0[:, 0:256], ACT.Sigmoid, scale=BIN_SCALE).then_inc(sem["bin_sigmoid"], 1)


def bin_pe(k, pe):
    sem, mm = k.sem, k.nc.tensor.matmul
    for s, sl in enumerate(k.slots):
        pe.wait_ge(sem["bin_qk"], nth(0, s))
        for j in range(TILES):
            last = mm(sl.b0[:, tok(j)], sl.d[:, 256 + j * P:256 + (j + 1) * P], sl.d[:, tok(j)], start=True, stop=True)
        last.then_inc(sem["bin_scores"], 1)
    for s, sl in enumerate(k.slots):
        pe.wait_ge(sem["bin_masked"], nth(0, s))
        for j in range(TILES):
            last = mm(sl.b1[:, tok(j)], sl.e[:, tok(j)], sl.b[:, tok(j)], start=True, stop=True)
        last.then_inc(sem["layer_out"], 1)


MHA_HEADS, MHA_D = 16, 8


def mha_context_pe(k, pe, L):
    mm, w = k.nc.tensor.matmul, k.w["mha"]
    for s, sl in enumerate(k.slots):
        if L:
            pe.wait_ge(k.sem["x_updated"], nth(L - 1, s))
        for j in range(TILES):
            mm(sl.b0[:, 256 + j * P:256 + (j + 1) * P], sl.ctxT[:, tok(j)], w["WkT"], start=True, stop=True)
        for b in range(SLOT_BATCHES):
            for h in range(HALVES):
                mm(sl.b1[h * SEQ:(h + 1) * SEQ, tok(b)], sl.ctxT[:, bat(b)], w["WvT"], start=True, stop=True)


def mha_pe(k, pe, n):
    sem, mm, w = k.sem, k.nc.tensor.matmul, k.w["mha"]
    for s, sl in enumerate(k.slots):
        pe.wait_ge(sem["ln_yT"], nth(n, s))
        for j in range(TILES):
            last = mm(sl.b0[:, tok(j)], sl.yT[:, tok(j)], w["WqT"], start=True, stop=True)
        last.then_inc(sem["projected"], 1)
    for s, sl in enumerate(k.slots):
        pe.wait_ge(sem["mha_qk"], nth(0, s))
        for j in range(2 * TILES):
            last = k.nc.tensor.transpose(sl.b0[:, tok(j)], sl.a[:, tok(j)], k.ident)
        last.then_inc(sem["mha_qkT_psum"], 1)
    for j in range(TILES):
        t = []
        for first in (0, 1):
            for s, sl in enumerate(k.slots):
                if first:
                    pe.wait_ge(k.pe_step.sem, t[s])
                else:
                    pe.wait_ge(sem["mha_kheads"], nth(0, s))
                    if j:
                        pe.wait_ge(sem["mha_out"], nth(j - 1, s))
                kh = sl.b[:, :].rearrange("p (h t) -> p h t", h=4)
                for b in range(HALVES * j, HALVES * j + HALVES):
                    for g in (first, first + 2):
                        r = slice(32 * g, 32 * g + 32)
                        last = mm(sl.ps[half(b), g // 2, first * 256:first * 256 + 256].rearrange("p (h t) -> p h t", h=4),
                                  sl.c[r, bat(b)], kh[r, :, bat(b)], start=True, stop=True,
                                  tile_position=(32 * g, (b % HALVES) * SEQ))
                if first:
                    last.then_inc(sem["mha_scores"], 1)
                else:
                    t.append(k.pe_step(last))
        for s, sl in enumerate(k.slots):
            pe.wait_ge(sem["mha_exp"], nth(j, s))
            for i in range(8):
                last = k.nc.tensor.transpose(sl.both[:, tok(i)], sl.d[:, tok(i)], k.ident)
            last.then_inc(sem["mha_probsT_psum"], 1)
        for s, sl in enumerate(k.slots):
            pe.wait_ge(sem["mha_probsT"], nth(j, s))
            for b in range(HALVES * j, HALVES * j + HALVES):
                for i in range(8):
                    last = mm(sl.b0[half(b), 16 * i:16 * i + 16],
                              sl.e[:, i * P + (b % 2) * SEQ:i * P + (b % 2) * SEQ + SEQ],
                              sl.a[:, 512 + b * P + 16 * i:512 + b * P + 16 * i + 16], start=True, stop=True)
            last.then_inc(sem["mha_heads"], 1)
    for s, sl in enumerate(k.slots):
        pe.wait_ge(sem["mha_out"], nth(TILES - 1, s))
        for j in range(TILES):
            last = k.nc.tensor.transpose(sl.b1[:, tok(j)], sl.a[:, tok(j)], k.ident)
        last.then_inc(sem["mha_outT_psum"], 1)
    for s, sl in enumerate(k.slots):
        pe.wait_ge(sem["mha_outT"], nth(0, s))
        for j in range(TILES):
            last = mm(sl.b0[:, tok(j)], sl.c[:, tok(j)], w["WoT"], start=True, stop=True)
        last.then_inc(sem["layer_out"], 1)


def mha_act(k, act):
    sem, a, w = k.sem, k.nc.scalar, k.w["mha"]
    for s, sl in enumerate(k.slots):
        act.wait_ge(sem["mha_qkT_psum"], nth(0, s))
        a.activation(sl.c[:, 0:512], sl.b0, ACT.Identity, bias=w["beta"], scale=w["gamma"]).then_inc(sem["mha_qkT"], 1)
    for j in range(TILES):
        for s, sl in enumerate(k.slots):
            act.wait_ge(sem["mha_shifted"], nth(j, s))
            a.activation(sl.d[:, :], sl.d[:, :], ACT.Exp, scale=MHA_D ** -0.5).then_inc(sem["mha_exp"], 1)
        for s, sl in enumerate(k.slots):
            act.wait_ge(sem["mha_probsT_psum"], nth(j, s))
            a.copy(sl.e[:, :], sl.both).then_inc(sem["mha_probsT"], 1)
    for s, sl in enumerate(k.slots):
        act.wait_ge(sem["mha_outT_psum"], nth(0, s))
        a.copy(sl.c[:, 0:256], sl.b1[:, 0:256]).then_inc(sem["mha_outT"], 1)


def mha_dve(k, dve, L):
    sem, v = k.sem, k.nc.vector
    t = []
    for s, sl in enumerate(k.slots):
        dve.wait_ge(sem["projected"], nth(k.projected_at["mha"], s))
        for j in range(2 * TILES):
            last = v.bn_stats(sl.stats[:, j, :], sl.b0[:, tok(j)])
        t.append(k.step(last))
    for s, sl in enumerate(k.slots):
        v.tensor_tensor(sl.a[:, 512:1024].rearrange("p (b c) -> p b c", b=SLOT_BATCHES), sl.b1.rearrange("p (b c) -> p b c", b=SLOT_BATCHES),
                        spread(k.const["parity8"], 1, SLOT_BATCHES), ALU.mult)
        dve.wait_ge(k.step.sem, t[s])
        for j in range(2 * TILES):
            last = v.bn_aggr(sl.mv[:, j, :], sl.stats[:, j, :])
        last.then_inc(sem["inner_stats"], 1)
    for s, sl in enumerate(k.slots):
        dve.wait_ge(sem["inner_rstd"], nth(k.inner_at["mha"], s))
        for j in range(2 * TILES):
            last = v.tensor_scalar(sl.a[:, tok(j)], sl.b0[:, tok(j)], sl.mv[:, j, 0:1], sl.rstd[:, j:j + 1],
                                   ALU.subtract, ALU.mult)
        last.then_inc(sem["mha_qk"], 1)
    for s, sl in enumerate(k.slots):
        dve.wait_ge(sem["mha_qkT"], nth(0, s))
        v.tensor_tensor(sl.b[:, :].rearrange("p (h t) -> p h t", h=4), spread(sl.c[:, 256:512], 1, 4),
                        spread(k.const["head_of_4"], 2, SLOT_TOKENS), ALU.mult).then_inc(sem["mha_kheads"], 1)
    for j in range(TILES):
        t = []
        for s, sl in enumerate(k.slots):
            dve.wait_ge(sem["mha_scores"], nth(j, s))
            t.append(k.step(v.tensor_reduce(sl.t[:, 0:16], sl.both.rearrange("p (h t) -> p h t", h=16), AX.X, ALU.max)))
            dve.wait_ge(k.step.sem, t[s])
            v.tensor_tensor(sl.d[:, :].rearrange("p (h t) -> p h t", h=16), sl.both.rearrange("p (h t) -> p h t", h=16),
                            spread(sl.t[:, 0:16], 2, SEQ), ALU.subtract).then_inc(sem["mha_shifted"], 1)
        for s, sl in enumerate(k.slots):
            dve.wait_ge(sem["mha_exp"], nth(j, s))
            t[s] = k.step(v.tensor_reduce(sl.t[:, 16:32], sl.d[:, :].rearrange("p (h t) -> p h t", h=16), AX.X, ALU.add))
            dve.wait_ge(k.step.sem, t[s])
            t[s] = k.step(v.reciprocal(sl.t[:, 32:48], sl.t[:, 16:32]))
        for s, sl in enumerate(k.slots):
            dve.wait_ge(k.step.sem, t[s])
            dve.wait_ge(sem["mha_heads"], nth(j, s))
            v.tensor_tensor(sl.a[:, tok(j)].rearrange("p (h e) -> p h e", h=16), sl.b0[:, 0:P].rearrange("p (h e) -> p h e", h=16),
                            spread(sl.t[:, 32:48], 2, MHA_D), ALU.mult).then_inc(sem["mha_out"], 1)
    add_to_x_dve(k, dve, L, "layer_out", k.out_at["mha"], 0)


def gate_view(ap, experts):
    return ap[:, 0:16].rearrange("p (t e) -> p t e", t=TILES)[:, :, 0:experts]


def gate_act(k, act, n):
    for s, sl in enumerate(k.slots):
        act.wait_ge(k.sem["gate_shifted"], nth(n, s))
        k.nc.scalar.activation(sl.g[:, 0:16], sl.g[:, 0:16], ACT.Exp).then_inc(k.sem["gate_exp"], 1)


def gate_dve(k, dve, n, experts):
    sem, v, step = k.sem, k.nc.vector, k.step
    before = k.const["before8" if experts == 8 else "before4"].rearrange("p (e f) -> p e f", e=experts)
    t = []
    for s, sl in enumerate(k.slots):
        dve.wait_ge(sem["gate_logits"], nth(n, s))
        t.append(step(v.tensor_reduce(sl.t[:, 0:2], gate_view(sl.b0, experts), AX.X, ALU.max)))
        dve.wait_ge(step.sem, t[s])
        v.tensor_tensor(gate_view(sl.g, experts), gate_view(sl.b0, experts), spread(sl.t[:, 0:2], 2, experts),
                        ALU.subtract).then_inc(sem["gate_shifted"], 1)
    for s, sl in enumerate(k.slots):
        dve.wait_ge(sem["gate_exp"], nth(n, s))
        t[s] = step(v.tensor_reduce(sl.t[:, 2:4], gate_view(sl.g, experts), AX.X, ALU.add))
        dve.wait_ge(step.sem, t[s])
        t[s] = step(v.reciprocal(sl.t[:, 4:6], sl.t[:, 2:4]))
        dve.wait_ge(step.sem, t[s])
        g = gate_view(sl.g, experts)
        t[s] = step(v.tensor_tensor(g, g, spread(sl.t[:, 4:6], 2, experts), ALU.mult))
    size = TILES * experts * experts
    for s, sl in enumerate(k.slots):
        dve.wait_ge(step.sem, t[s])
        for j in range(TILES):
            g = gate_view(sl.g, experts)[:, j, :]
            c = slice(j * experts * experts, (j + 1) * experts * experts)
            for dst, op in ((sl.a, ALU.is_gt), (sl.b, ALU.is_ge)):
                last = v.tensor_tensor(dst[:, c].rearrange("p (e f) -> p e f", e=experts), spread(g, 1, experts),
                                       spread(g, 2, experts), op)
        t[s] = step(last)
        dve.wait_ge(step.sem, t[s])
        eq = sl.b[:, 0:size].rearrange("p (t e f) -> p t e f", t=TILES, e=experts)
        t[s] = step(v.tensor_tensor(eq, eq, spread(before, 1, TILES), ALU.mult))
        dve.wait_ge(step.sem, t[s])
        t[s] = step(v.tensor_tensor(sl.a[:, 0:size], sl.a[:, 0:size], sl.b[:, 0:size], ALU.max))
        dve.wait_ge(step.sem, t[s])
        sel = sl.g[:, 16:32].rearrange("p (t e) -> p t e", t=TILES)[:, :, 0:experts]
        t[s] = step(v.tensor_reduce(sel, sl.a[:, 0:size].rearrange("p (t e f) -> p t e f", t=TILES, e=experts), AX.X, ALU.add))
        dve.wait_ge(step.sem, t[s])
        sel = sl.g[:, 16:32].rearrange("p (t e) -> p t e", t=TILES)[:, :, 0:experts]
        t[s] = step(v.tensor_scalar(sel, sel, 2.0, None, ALU.is_lt))
    return t


def weightsT_pe(k, pe, s, sl, n, w, count):
    pe.wait_ge(k.sem["gate_weights"], nth(n, s))
    for j in range(TILES):
        last = k.nc.tensor.transpose(sl.b1[0:count, tok(j)], w[:, j, :], k.ident)
    last.then_inc(k.sem["gate_wT_psum"], 1)


def weightsT_act(k, act, n, count, scale):
    for s, sl in enumerate(k.slots):
        act.wait_ge(k.sem["gate_wT_psum"], nth(n, s))
        k.nc.scalar.activation(sl.wT[0:count, :], sl.b1[0:count, 0:SLOT_TOKENS], ACT.Copy,
                               scale=scale).then_inc(k.sem["gate_wT"], 1)


FF = 4


def added(k, first):
    return first - 1 if first else 0


def nets_pe(k, pe, w, nets, first, n_gate, weights, count):
    sem, mm = k.sem, k.nc.tensor.matmul
    for e in range(nets):
        for s, sl in enumerate(k.slots):
            if e == 0:
                pe.wait_ge(sem["gate_shifted"], nth(n_gate, s))
            else:
                pe.wait_ge(sem["moe_added"], nth(added(k, first) + e - 1, s))
            for f in range(FF):
                last = mm(sl.both[:, f * 256:(f + 1) * 256], w[f"W1_{e}"][:, f * P:(f + 1) * P], sl.yT[:, :],
                          start=True, stop=True)
                if f == 1:
                    last.then_inc(sem["moe_h"], 1)
                if f == 3:
                    last.then_inc(sem["moe_h2"], 1)
        if e == 0:
            for s, sl in enumerate(k.slots):
                pe.wait_ge(sem["moe_act"], nth(first, s))
                pe.wait_ge(sem["moe_act2"], nth(first, s))
                weightsT_pe(k, pe, s, sl, n_gate, weights(sl), count)
        for s, sl in enumerate(k.slots):
            pe.wait_ge(sem["moe_act"], nth(first + e, s))
            pe.wait_ge(sem["moe_act2"], nth(first + e, s))
            if e == 0:
                pe.wait_ge(sem["gate_wT"], nth(n_gate, s))
            for j in range(TILES):
                for f in range(FF):
                    last = mm(sl.b0[:, tok(j)], sl.e[:, f * 256 + j * P:f * 256 + (j + 1) * P],
                              w[f"W2_{e}"][:, f * P:(f + 1) * P], start=(f == 0), stop=(f == FF - 1 and e > 0))
                if e == 0:
                    last = mm(sl.b0[:, tok(j)], sl.wT[0:count, tok(j)], w["b2"], start=False, stop=True)
            last.then_inc(sem["moe_y"], 1)


def nets_add_dve(k, dve, L, e, nets, first, weight):
    sem, v = k.sem, k.nc.vector
    for s, sl in enumerate(k.slots):
        dve.wait_ge(sem["moe_y"], nth(first + e, s))
        if e:
            dve.wait_ge(sem["moe_added"], nth(added(k, first) + e - 1, s))
        for j in range(TILES):
            last = v.scalar_tensor_tensor(out=sl.x[:, j, :], in0=sl.b0[:, tok(j)], scalar=weight(sl, j),
                                          in1=sl.x[:, j, :], op0=ALU.mult, op1=ALU.add)
        last.then_inc(sem["moe_added" if e < nets - 1 else "x_updated"], 1)
        if e == nets - 1:
            statistics_dve(k, dve, L + 1, s, sl)


MOE_NETS = 9


def moe_pe(k, pe, n, n_gate):
    sem, mm, w = k.sem, k.nc.tensor.matmul, k.w["moe"]
    for s, sl in enumerate(k.slots):
        pe.wait_ge(sem["ln_yT"], nth(n, s))
        mm(sl.b1[0:32, 0:256], w["Wr1"], sl.yT[:, :], start=True, stop=True).then_inc(sem["moe_router"], 1)
    for s, sl in enumerate(k.slots):
        pe.wait_ge(sem["moe_relu"], nth(0, s))
        for j in range(TILES):
            mm(sl.b0[:, 8 * j:8 * j + 8], sl.c[0:32, tok(j)], w["Wr2"], start=True, stop=False)
            last = mm(sl.b0[:, 8 * j:8 * j + 8], k.ones[0:1, :], w["br2"], start=False, stop=True)
        last.then_inc(sem["gate_logits"], 1)
    nets_pe(k, pe, w, MOE_NETS, 0, n_gate, lambda sl: sl.w[:, :, :], 9)


def moe_act(k, act, n_gate):
    sem, a, w = k.sem, k.nc.scalar, k.w["moe"]
    for s, sl in enumerate(k.slots):
        act.wait_ge(sem["moe_router"], nth(0, s))
        a.activation(sl.c[0:32, 0:256], sl.b1[0:32, 0:256], ACT.Relu, bias=w["br1"]).then_inc(sem["moe_relu"], 1)
    gate_act(k, act, n_gate)

    def hidden(e):
        for s, sl in enumerate(k.slots):
            for f in range(FF):
                if f % 2 == 0:
                    act.wait_ge(sem["moe_h2" if f else "moe_h"], nth(e, s))
                last = a.activation(sl.e[:, f * 256:(f + 1) * 256], sl.both[:, f * 256:(f + 1) * 256], ACT.Silu,
                                    bias=w["b1"][:, e * FF + f:e * FF + f + 1])
                if f == 1:
                    last.then_inc(sem["moe_act"], 1)
                if f == 3:
                    last.then_inc(sem["moe_act2"], 1)
    hidden(0)
    for s, sl in enumerate(k.slots):
        act.wait_ge(sem["gate_top"], nth(0, s))
        a.activation(sl.g[:, 32:48], sl.g[:, 32:48], ACT.Exp, scale=0.5).then_inc(sem["gate_expw"], 1)
    weightsT_act(k, act, n_gate, 9, 1.0)
    for e in range(1, MOE_NETS):
        hidden(e)


def moe_dve(k, dve, L, n_gate):
    sem, v, step = k.sem, k.nc.vector, k.step
    t = gate_dve(k, dve, n_gate, 8)
    for s, sl in enumerate(k.slots):
        v.tensor_tensor(gate_view(sl.g[:, 32:48], 8), gate_view(sl.g, 8), spread(sl.t[:, 4:6], 2, 8),
                        ALU.subtract).then_inc(sem["gate_top"], 1)
    for s, sl in enumerate(k.slots):
        dve.wait_ge(step.sem, t[s])
        dve.wait_ge(sem["gate_expw"], nth(0, s))
        t[s] = step(v.tensor_tensor(sl.g[:, 32:48], sl.g[:, 32:48], sl.g[:, 16:32], ALU.mult))
        dve.wait_ge(step.sem, t[s])
        t[s] = step(v.tensor_reduce(sl.t[:, 6:8], gate_view(sl.g[:, 32:48], 8), AX.X, ALU.add))
        dve.wait_ge(step.sem, t[s])
        t[s] = step(v.reciprocal(sl.t[:, 8:10], sl.t[:, 6:8]))
        dve.wait_ge(step.sem, t[s])
        v.tensor_tensor(sl.w[:, :, 0:8], gate_view(sl.g[:, 32:48], 8), spread(sl.t[:, 8:10], 2, 8),
                        ALU.mult).then_inc(sem["gate_weights"], 1)
    for e in range(MOE_NETS):
        nets_add_dve(k, dve, L, e, MOE_NETS, 0, lambda sl, j: 1.0 if e == 0 else sl.w[:, j, e - 1:e])


FFN_NETS, FFN_SHARED = 6, 2


def ffn_pe(k, pe, n, n_gate):
    sem, mm, w = k.sem, k.nc.tensor.matmul, k.w["ffn"]
    for s, sl in enumerate(k.slots):
        pe.wait_ge(sem["ln_yT"], nth(n, s))
        for j in range(TILES):
            mm(sl.b0[:, 8 * j:8 * j + 4], sl.yT[:, tok(j)], w["gate"], start=True, stop=False)
            last = mm(sl.b0[:, 8 * j:8 * j + 4], k.ones[0:1, :], w["gb"], start=False, stop=True)
        last.then_inc(sem["gate_logits"], 1)
    nets_pe(k, pe, w, FFN_NETS, k.moe_first["ffn"], n_gate, lambda sl: sl.w6[:, :, :], 6)


def ffn_act(k, act, n_gate):
    sem, a, w = k.sem, k.nc.scalar, k.w["ffn"]
    gate_act(k, act, n_gate)
    for e in range(FFN_NETS):
        for s, sl in enumerate(k.slots):
            act.wait_ge(sem["moe_h"], nth(k.moe_first["ffn"] + e, s))
            for f in range(2):
                last = a.activation(sl.e[:, f * 256:(f + 1) * 256], sl.both[:, f * 256:(f + 1) * 256], ACT.Relu,
                                    bias=w["b1"][:, e * FF + f:e * FF + f + 1])
            last.then_inc(sem["moe_act"], 1)
        if e == 0:
            weightsT_act(k, act, n_gate, 6, float(FFN_SHARED))


def ffn_dve(k, dve, L, n_gate):
    sem, v, w, first = k.sem, k.nc.vector, k.w["ffn"], k.moe_first["ffn"]
    t = gate_dve(k, dve, n_gate, 4)
    for s, sl in enumerate(k.slots):
        dve.wait_ge(k.step.sem, t[s])
        v.tensor_tensor(sl.w6[:, :, 0:4], gate_view(sl.g, 4), gate_view(sl.g[:, 16:32], 4),
                        ALU.mult).then_inc(sem["gate_weights"], 1)
    for e in range(FFN_NETS):
        for s, sl in enumerate(k.slots):
            dve.wait_ge(sem["moe_h2"], nth(first + e, s))
            for f in range(2, FF):
                last = v.tensor_scalar(sl.e[:, f * 256:(f + 1) * 256], sl.both[:, f * 256:(f + 1) * 256],
                                       w["b1"][:, e * FF + f:e * FF + f + 1], 0.0, ALU.add, ALU.max)
            last.then_inc(sem["moe_act2"], 1)
        nets_add_dve(k, dve, L, e, FFN_NETS, first,
                     lambda sl, j: 1.0 / FFN_SHARED if e < FFN_SHARED else sl.w6[:, j, e - FFN_SHARED:e - FFN_SHARED + 1])


def fst_pe(k, pe, n, n_gate):
    sem, mm, w = k.sem, k.nc.tensor.matmul, k.w["fst"]
    for s, sl in enumerate(k.slots):
        pe.wait_ge(sem["ln_yT"], nth(n, s))
        for j in range(TILES):
            last = mm(sl.b0[:, 8 * j:8 * j + 8], sl.yT[:, tok(j)], w["gate"], start=True, stop=True)
        last.then_inc(sem["gate_logits"], 1)
    for s, sl in enumerate(k.slots):
        pe.wait_ge(sem["gate_shifted"], nth(n_gate, s))
        for f in range(4):
            last = mm(sl.both[:, f * 256:(f + 1) * 256], w["W1"][:, f * P:(f + 1) * P], sl.yT[:, :], start=True, stop=True)
        last.then_inc(sem["fst_h"], 1)
    for s, sl in enumerate(k.slots):
        pe.wait_ge(sem["fst_gelu"], nth(0, s))
        weightsT_pe(k, pe, s, sl, n_gate, sl.w[:, :, 0:8], 8)
    for s, sl in enumerate(k.slots):
        pe.wait_ge(sem["gate_wT"], nth(n_gate, s))
        for f in range(4):
            last = mm(sl.both[:, f * 256:(f + 1) * 256], k.const["rows_of_8"][:, f * P:(f + 1) * P], sl.wT[0:8, :],
                      start=True, stop=True)
        last.then_inc(sem["fst_wb"], 1)
    for s, sl in enumerate(k.slots):
        pe.wait_ge(sem["fst_hw"], nth(0, s))
        for j in range(TILES):
            for f in range(4):
                mm(sl.b0[:, tok(j)], sl.e[:, f * 256 + j * P:f * 256 + (j + 1) * P], w["W2"][:, f * P:(f + 1) * P],
                   start=(f == 0), stop=False)
            last = mm(sl.b0[:, tok(j)], sl.wT[0:8, tok(j)], w["b2"], start=False, stop=True)
        last.then_inc(sem["layer_out"], 1)


def fst_act(k, act, n_gate):
    sem, a, w = k.sem, k.nc.scalar, k.w["fst"]
    gate_act(k, act, n_gate)
    for s, sl in enumerate(k.slots):
        act.wait_ge(sem["fst_h"], nth(0, s))
        for f in range(4):
            last = a.activation(sl.e[:, f * 256:(f + 1) * 256], sl.both[:, f * 256:(f + 1) * 256], ACT.Gelu,
                                bias=w["b1"][:, f:f + 1])
        last.then_inc(sem["fst_gelu"], 1)
    weightsT_act(k, act, n_gate, 8, 1.0)


def fst_dve(k, dve, L, n_gate):
    sem, v, step = k.sem, k.nc.vector, k.step
    t = gate_dve(k, dve, n_gate, 8)
    for s, sl in enumerate(k.slots):
        dve.wait_ge(step.sem, t[s])
        t[s] = step(v.tensor_tensor(sl.g[:, 32:48], sl.g[:, 0:16], sl.g[:, 16:32], ALU.mult))
        dve.wait_ge(step.sem, t[s])
        t[s] = step(v.tensor_reduce(sl.t[:, 6:8], gate_view(sl.g[:, 32:48], 8), AX.X, ALU.add))
        dve.wait_ge(step.sem, t[s])
        v.tensor_tensor(sl.w[:, :, 0:8], gate_view(sl.g[:, 16:32], 8), spread(sl.t[:, 6:8], 2, 8),
                        ALU.mult).then_inc(sem["gate_weights"], 1)
    for s, sl in enumerate(k.slots):
        dve.wait_ge(sem["fst_wb"], nth(0, s))
        v.tensor_tensor(sl.e[:, :], sl.e[:, :], sl.both, ALU.mult).then_inc(sem["fst_hw"], 1)
    add_to_x_dve(k, dve, L, "layer_out", k.out_at["fst"], 0)


def lin_pe(k, pe, n):
    sem, mm, w = k.sem, k.nc.tensor.matmul, k.w["lin"]
    for s, sl in enumerate(k.slots):
        pe.wait_ge(sem["ln_yT"], nth(n, s))
        mm(sl.b0[:, 0:256], w["WqT"], sl.yT[:, :], start=True, stop=True)
        mm(sl.b0[0:8, 256:512], w["Wg1T"], sl.yT[:, :], start=True, stop=True)
        for j in range(TILES):
            mm(sl.b1[:, 256 + j * P:256 + (j + 1) * P], sl.yT[:, tok(j)], w["WvT"], start=True, stop=True)
        mm(sl.b1[:, 0:256], w["WkT"], sl.yT[:, :], start=True, stop=True).then_inc(sem["projected"], 1)
    for s, sl in enumerate(k.slots):
        pe.wait_ge(sem["lin_kexp"], nth(0, s))
        pe.wait_ge(sem["lin_silu"], nth(0, s))
        for j in range(TILES):
            k.nc.tensor.transpose(sl.b0[:, tok(j)], sl.b[:, tok(j)], k.ident)
        mm(sl.b0[:, 256:512], w["Wg2T"], sl.d[0:8, 0:256], start=True, stop=True).then_inc(sem["lin_kt_psum"], 1)
    for s, sl in enumerate(k.slots):
        pe.wait_ge(sem["lin_kt"], nth(0, s))
        pe.wait_ge(sem["lin_v"], nth(0, s))
        pe.wait_ge(sem["lin_gate"], nth(0, s))
        for b in range(SLOT_BATCHES):
            j = b // HALVES
            last = mm(sl.ps[:, b % HALVES, tok(j)], sl.c[half(b), tok(j)], sl.c[half(b), 256 + j * P:256 + (j + 1) * P],
                      start=True, stop=True)
        last.then_inc(sem["lin_kv"], 1)
    for s, sl in enumerate(k.slots):
        pe.wait_ge(sem["lin_kvm"], nth(0, s))
        for b in range(SLOT_BATCHES):
            last = mm(sl.b0[half(b), tok(b // HALVES)], sl.a[:, bat(b)], sl.e[:, tok(b)], start=True, stop=True)
        last.then_inc(sem["lin_out"], 1)
    for s, sl in enumerate(k.slots):
        pe.wait_ge(sem["lin_n"], nth(0, s))
        for j in range(TILES):
            last = k.nc.tensor.transpose(sl.b1[:, tok(j)], sl.a[:, 256 + j * P:256 + (j + 1) * P], k.ident)
        last.then_inc(sem["lin_nT_psum"], 1)
    for s, sl in enumerate(k.slots):
        pe.wait_ge(sem["lin_gated"], nth(0, s))
        for j in range(TILES):
            last = mm(sl.b0[:, tok(j)], sl.b[:, 512 + j * P:512 + (j + 1) * P], w["WoT"], start=True, stop=True)
        last.then_inc(sem["layer_out"], 1)


def lin_act(k, act):
    sem, a, w = k.sem, k.nc.scalar, k.w["lin"]
    for s, sl in enumerate(k.slots):
        act.wait_ge(sem["projected"], nth(k.projected_at["lin"], s))
        a.activation(sl.d[0:8, 0:256], sl.b0[0:8, 256:512], ACT.Identity, bias=w["bg1"])
        a.activation(sl.a[:, 0:256], sl.b0[:, 0:256], ACT.Silu, bias=w["bq"]).then_inc(sem["lin_silu"], 1)
    for s, sl in enumerate(k.slots):
        act.wait_ge(sem["lin_kshift"], nth(0, s))
        a.activation(sl.b[:, 0:256], sl.b[:, 0:256], ACT.Exp).then_inc(sem["lin_kexp"], 1)
    for s, sl in enumerate(k.slots):
        act.wait_ge(sem["lin_kt_psum"], nth(0, s))
        a.copy(sl.c[:, 0:256], sl.b0[:, 0:256]).then_inc(sem["lin_kt"], 1)
    for s, sl in enumerate(k.slots):
        a.activation(sl.d[:, 256:512], sl.b0[:, 256:512], ACT.Sigmoid, bias=w["bg2"]).then_inc(sem["lin_gate"], 1)


def lin_dve(k, dve, L):
    sem, v, w, step = k.sem, k.nc.vector, k.w["lin"], k.step
    t = []
    for s, sl in enumerate(k.slots):
        dve.wait_ge(sem["projected"], nth(k.projected_at["lin"], s))
        t.append(step(v.tensor_scalar(sl.b[:, 256:512], sl.b1[:, 0:256], w["bk"], None, ALU.add)))
    for s, sl in enumerate(k.slots):
        v.tensor_tensor(sl.c[:, 256:512].rearrange("p (t c) -> p t c", t=TILES), sl.b1[:, 256:512].rearrange("p (t c) -> p t c", t=TILES),
                        spread(w["bv"], 1, TILES), ALU.add).then_inc(sem["lin_v"], 1)
        dve.wait_ge(step.sem, t[s])
        t[s] = step(v.tensor_reduce(sl.t[:, 0:4], sl.b[:, 256:512].rearrange("p (b t) -> p b t", b=SLOT_BATCHES), AX.X, ALU.max))
        dve.wait_ge(step.sem, t[s])
        v.tensor_tensor(sl.b[:, 0:256].rearrange("p (b t) -> p b t", b=SLOT_BATCHES),
                        sl.b[:, 256:512].rearrange("p (b t) -> p b t", b=SLOT_BATCHES),
                        spread(sl.t[:, 0:4], 2, SEQ), ALU.subtract).then_inc(sem["lin_kshift"], 1)
    for s, sl in enumerate(k.slots):
        dve.wait_ge(sem["lin_kexp"], nth(0, s))
        t[s] = step(v.tensor_reduce(sl.t[:, 4:8], sl.b[:, 0:256].rearrange("p (b t) -> p b t", b=SLOT_BATCHES), AX.X, ALU.add))
        dve.wait_ge(step.sem, t[s])
        t[s] = step(v.reciprocal(sl.t[:, 8:12], sl.t[:, 4:8]))
    for s, sl in enumerate(k.slots):
        dve.wait_ge(step.sem, t[s])
        dve.wait_ge(sem["lin_kv"], nth(0, s))
        for b in range(SLOT_BATCHES):
            last = v.scalar_tensor_tensor(out=sl.e[:, tok(b)], in0=sl.ps[:, b % HALVES, tok(b // HALVES)], scalar=sl.t[:, 8 + b:9 + b],
                                          in1=k.const["diag8"], op0=ALU.mult, op1=ALU.mult)
        last.then_inc(sem["lin_kvm"], 1)
    for s, sl in enumerate(k.slots):
        dve.wait_ge(sem["lin_out"], nth(0, s))
        for j in range(TILES):
            last = v.bn_stats(sl.stats[:, j, :], sl.b0[:, tok(j)])
        t[s] = step(last)
        dve.wait_ge(step.sem, t[s])
        for j in range(TILES):
            last = v.bn_aggr(sl.mv[:, j, :], sl.stats[:, j, :])
        last.then_inc(sem["inner_stats"], 1)
    for s, sl in enumerate(k.slots):
        dve.wait_ge(sem["inner_rstd"], nth(k.inner_at["lin"], s))
        for j in range(TILES):
            last = v.tensor_scalar(sl.a[:, 256 + j * P:256 + (j + 1) * P], sl.b0[:, tok(j)], sl.mv[:, j, 0:1],
                                   sl.rstd[:, j:j + 1], ALU.subtract, ALU.mult)
        last.then_inc(sem["lin_n"], 1)
    for s, sl in enumerate(k.slots):
        dve.wait_ge(sem["lin_nT_psum"], nth(0, s))
        t[s] = step(v.tensor_scalar(sl.b[:, 512:768], sl.b1[:, 0:256], w["gamma"], w["beta"], ALU.mult, ALU.add))
        dve.wait_ge(step.sem, t[s])
        v.tensor_tensor(sl.b[:, 512:768], sl.b[:, 512:768], sl.d[:, 256:512], ALU.mult).then_inc(sem["lin_gated"], 1)
    add_to_x_dve(k, dve, L, "layer_out", k.out_at["lin"], 0)


ONE_SCALE = D ** -0.5


def one_context_pe(k, pe, L):
    mm, w = k.nc.tensor.matmul, k.w["one"]
    for s, sl in enumerate(k.slots):
        if L:
            pe.wait_ge(k.sem["x_updated"], nth(L - 1, s))
        mm(sl.b0[:, 256:512], w["Wk"], sl.ctxT[:, :], start=True, stop=True)
        for j in range(TILES):
            mm(sl.b1[:, tok(j)], sl.ctxT[:, tok(j)], w["Wv"], start=True, stop=True)


def one_pe(k, pe, n):
    sem, mm, w = k.sem, k.nc.tensor.matmul, k.w["one"]
    for s, sl in enumerate(k.slots):
        pe.wait_ge(sem["ln_yT"], nth(n, s))
        mm(sl.b0[:, 0:256], w["Wq"], sl.yT[:, :], start=True, stop=True).then_inc(sem["projected"], 1)
    for s, sl in enumerate(k.slots):
        pe.wait_ge(sem["one_qk"], nth(0, s))
        for b in range(SLOT_BATCHES):
            last = mm(sl.b0[half(b), (b // HALVES) * SEQ:(b // HALVES + 1) * SEQ], sl.a[:, bat(b)],
                      sl.a[:, 256 + b * SEQ:256 + (b + 1) * SEQ], start=True, stop=True)
        last.then_inc(sem["one_scores"], 1)
    for s, sl in enumerate(k.slots):
        pe.wait_ge(sem["one_probs"], nth(0, s))
        pe.wait_ge(sem["one_v"], nth(0, s))
        for j in range(TILES):
            last = k.nc.tensor.transpose(sl.b1[:, tok(j)], sl.d[:, tok(j)], k.ident)
        last.then_inc(sem["one_PT_psum"], 1)
    for s, sl in enumerate(k.slots):
        pe.wait_ge(sem["one_PT"], nth(0, s))
        for j in range(TILES):
            last = mm(sl.b0[:, tok(j)], sl.c[:, tok(j)], sl.b[:, tok(j)], start=True, stop=True)
        last.then_inc(sem["layer_out"], 1)


def one_act(k, act):
    sem, a = k.sem, k.nc.scalar
    for s, sl in enumerate(k.slots):
        act.wait_ge(sem["projected"], nth(k.projected_at["one"], s))
        a.copy(sl.a[:, 0:512], sl.b0).then_inc(sem["one_qk"], 1)
    for s, sl in enumerate(k.slots):
        act.wait_ge(sem["one_max"], nth(0, s))
        for j in range(TILES):
            for h in range(HALVES):
                r = slice(h * SEQ, (h + 1) * SEQ)
                last = a.activation(sl.d[r, j * P + h * SEQ:j * P + (h + 1) * SEQ], sl.b0[r, j * SEQ:(j + 1) * SEQ], ACT.Exp, bias=sl.t[r, 2 + j:3 + j],
                                    scale=ONE_SCALE, accum_out=sl.t[r, 4 + j:5 + j])
        last.then_inc(sem["one_probs"], 1)
    for s, sl in enumerate(k.slots):
        act.wait_ge(sem["one_PT_psum"], nth(0, s))
        a.copy(sl.c[:, 0:256], sl.b1[:, 0:256]).then_inc(sem["one_PT"], 1)


def one_dve(k, dve, L):
    sem, v, step = k.sem, k.nc.vector, k.step
    t = []
    for s, sl in enumerate(k.slots):
        dve.wait_ge(sem["projected"], nth(k.projected_at["one"], s))
        v.memset(sl.d[:, 0:256], 0.0)
        v.tensor_copy(sl.b[:, 0:256], sl.b1[:, 0:256]).then_inc(sem["one_v"], 1)
    for s, sl in enumerate(k.slots):
        dve.wait_ge(sem["one_scores"], nth(0, s))
        t.append(step(v.tensor_reduce(sl.t[:, 0:2], sl.b0[:, 0:P].rearrange("p (t q) -> p t q", t=TILES), AX.X, ALU.max)))
        dve.wait_ge(step.sem, t[s])
        v.tensor_scalar(sl.t[:, 2:4], sl.t[:, 0:2], -ONE_SCALE, None, ALU.mult).then_inc(sem["one_max"], 1)
    for s, sl in enumerate(k.slots):
        dve.wait_ge(sem["one_probs"], nth(0, s))
        t[s] = step(v.reciprocal(sl.t[:, 6:8], sl.t[:, 4:6]))
    for s, sl in enumerate(k.slots):
        dve.wait_ge(step.sem, t[s])
        dve.wait_ge(sem["layer_out"], nth(k.out_at["one"], s))
        for j in range(TILES):
            last = v.scalar_tensor_tensor(out=sl.x[:, j, :], in0=sl.b0[:, tok(j)], scalar=sl.t[:, 6 + j:7 + j],
                                          in1=sl.x[:, j, :], op0=ALU.mult, op1=ALU.add)
        last.then_inc(sem["x_updated"], 1)
        statistics_dve(k, dve, L + 1, s, sl)


TREE_DEPTH, LEAVES = 8, 256


def tree_pe(k, pe, n):
    sem, mm, w = k.sem, k.nc.tensor.matmul, k.w["tree"]
    for s, sl in enumerate(k.slots):
        pe.wait_ge(sem["ln_yT"], nth(n, s))
        mm(sl.b0[:, 0:256], w["WqT"], sl.yT[:, :], start=True, stop=True).then_inc(sem["projected"], 1)
    for s, sl in enumerate(k.slots):
        pe.wait_ge(sem["tree_q"], nth(0, s))
        for j in range(TILES):
            last = mm(sl.b1[:, j * LEAVES:(j + 1) * LEAVES], sl.a[:, tok(j)], w["routersT"], start=True, stop=True)
        last.then_inc(sem["tree_logit"], 1)
    for s, sl in enumerate(k.slots):
        pe.wait_ge(sem["tree_leaf"], nth(0, s))
        for h in range(2):
            for j in range(TILES):
                last = k.nc.tensor.transpose(sl.b0[:, h * 256 + j * P:h * 256 + (j + 1) * P],
                                             sl.c[:, j * LEAVES + h * P:j * LEAVES + (h + 1) * P], k.ident)
        last.then_inc(sem["tree_leafT_psum"], 1)
    for s, sl in enumerate(k.slots):
        pe.wait_ge(sem["tree_leafT"], nth(0, s))
        for h in range(2):
            last = mm(sl.b1[:, 0:256], w["leaves"][:, h * P:(h + 1) * P], sl.d[:, h * 256:(h + 1) * 256],
                      start=(h == 0), stop=(h == 1))
        last.then_inc(sem["tree_ret"], 1)
    for s, sl in enumerate(k.slots):
        pe.wait_ge(sem["tree_rT"], nth(0, s))
        for j in range(TILES):
            last = mm(sl.b0[:, tok(j)], sl.a[:, 256 + j * P:256 + (j + 1) * P], w["WoT"], start=True, stop=True)
        last.then_inc(sem["layer_out"], 1)


def tree_act(k, act):
    sem, a = k.sem, k.nc.scalar
    for s, sl in enumerate(k.slots):
        act.wait_ge(sem["projected"], nth(k.projected_at["tree"], s))
        a.copy(sl.a[:, 0:256], sl.b0[:, 0:256]).then_inc(sem["tree_q"], 1)
    for s, sl in enumerate(k.slots):
        act.wait_ge(sem["tree_logit"], nth(0, s))
        a.activation(sl.b[:, :].rearrange("p (n r) -> p n r", r=2)[:, :, 1], sl.b1, ACT.Sigmoid).then_inc(sem["tree_gate"], 1)
    for s, sl in enumerate(k.slots):
        act.wait_ge(sem["tree_leafT_psum"], nth(0, s))
        a.copy(sl.d[:, 0:512], sl.b0).then_inc(sem["tree_leafT"], 1)
    for s, sl in enumerate(k.slots):
        act.wait_ge(sem["tree_ret"], nth(0, s))
        a.copy(sl.a[:, 256:512], sl.b1[:, 0:256]).then_inc(sem["tree_rT"], 1)


def tree_dve(k, dve, L):
    sem, v, step = k.sem, k.nc.vector, k.step
    t = []
    for s, sl in enumerate(k.slots):
        dve.wait_ge(sem["tree_gate"], nth(0, s))
        gates = sl.b[:, :].rearrange("p (n r) -> p n r", r=2)
        t.append(step(v.tensor_scalar(gates[:, :, 0], gates[:, :, 1], -1.0, 1.0, ALU.mult, ALU.add)))
    for level in range(1, TREE_DEPTH):
        nodes = 2 ** level
        for s, sl in enumerate(k.slots):
            gates = sl.b[:, :].rearrange("p (t n r) -> p t n r", t=TILES, r=2)
            if level == 1:
                prev = gates[:, :, 0, :]
            else:
                prev = (sl.c, sl.e)[level % 2][:, 0:512].rearrange("p (t n) -> p t n", t=TILES)[:, :, 0:nodes]
            out = (sl.e, sl.c)[level % 2][:, 0:512].rearrange("p (t n r) -> p t n r", t=TILES, r=2)[:, :, 0:nodes, :]
            dve.wait_ge(step.sem, t[s])
            for j in range(TILES):
                last = v.tensor_tensor(out[:, j], spread(prev[:, j], 2, 2), gates[:, j, nodes - 1:2 * nodes - 1, :], ALU.mult)
            if level < TREE_DEPTH - 1:
                t[s] = step(last)
            else:
                last.then_inc(sem["tree_leaf"], 1)
    add_to_x_dve(k, dve, L, "layer_out", k.out_at["tree"], 0)


LHA_HEADS, LHA_D = 8, 64
LHA_SCALE = LHA_D ** -0.5


def by64(ap):
    return ap.rearrange("p (h t) -> p h t", t=64)


def lha_pe(k, pe, n):
    sem, mm, w = k.sem, k.nc.tensor.matmul, k.w["lha"]
    for s, sl in enumerate(k.slots):
        pe.wait_ge(sem["ln_yT"], nth(n, s))
        for c in range(4):
            last = mm(sl.both[:, c * 256:(c + 1) * 256], w["Wk"][:, c * P:(c + 1) * P], sl.yT[:, :], start=True, stop=True)
        last.then_inc(sem["projected"], 1)
    for s, sl in enumerate(k.slots):
        pe.wait_ge(sem["lha_kshift"], nth(0, s))
        for j in range(TILES):
            last = mm(sl.ps[:, j, :], sl.yT[:, tok(j)], w["Wq"], start=True, stop=True)
        last.then_inc(sem["lha_q_psum"], 1)
    for s, sl in enumerate(k.slots):
        pe.wait_ge(sem["lha_qshift"], nth(0, s))
        for j in range(TILES):
            last = mm(sl.ps[:, j, :], sl.yT[:, tok(j)], w["Wv"], start=True, stop=True)
        last.then_inc(sem["lha_v_psum"], 1)
    for s, sl in enumerate(k.slots):
        pe.wait_ge(sem["lha_kexp"], nth(0, s))
        pe.wait_ge(sem["lha_v"], nth(0, s))
        for j in range(TILES):
            for c in range(4):
                last = k.nc.tensor.transpose(sl.ps[:, j, tok(c)], sl.a[:, c * 256 + j * P:c * 256 + (j + 1) * P], k.ident)
        last.then_inc(sem["lha_kt_psum"], 1)
    for s, sl in enumerate(k.slots):
        pe.wait_ge(sem["lha_qn"], nth(0, s))
        pe.wait_ge(sem["lha_kt"], nth(0, s))
        for c in range(4):
            for j in range(TILES):
                last = k.nc.tensor.transpose(sl.both[:, c * 256 + j * P:c * 256 + (j + 1) * P],
                                             sl.c[:, j * 512 + c * P:j * 512 + (c + 1) * P], k.ident)
        last.then_inc(sem["lha_qT_psum"], 1)
    for j in range(TILES):
        for s, sl in enumerate(k.slots):
            pe.wait_ge(sem["lha_qT"], nth(0, s))
            if j:
                pe.wait_ge(sem["lha_oT"], nth(j - 1, s))
            for h in range(HALVES):
                r = slice(h * SEQ, (h + 1) * SEQ)
                for c in range(4):
                    last = mm(sl.ps[:, h, tok(c)], sl.b[r, j * 512 + c * P:j * 512 + (c + 1) * P],
                              sl.d[r, j * 512 + c * P:j * 512 + (c + 1) * P], start=True, stop=True)
            last.then_inc(sem["lha_kv"], 1)
        for s, sl in enumerate(k.slots):
            pe.wait_ge(sem["lha_kvm"], nth(j, s))
            for c in range(4):
                for h in range(HALVES):
                    last = mm(sl.b0[:, c * P + h * SEQ:c * P + (h + 1) * SEQ], sl.e[:, h * 512 + c * P:h * 512 + (c + 1) * P],
                              sl.a[:, c * 256 + j * P + h * SEQ:c * 256 + j * P + (h + 1) * SEQ], start=True, stop=True)
            last.then_inc(sem["lha_oT_psum"], 1)
    for s, sl in enumerate(k.slots):
        pe.wait_ge(sem["lha_oT"], nth(TILES - 1, s))
        for j in range(TILES):
            for c in range(4):
                last = mm(sl.b1[:, tok(j)], sl.c[:, j * 512 + c * P:j * 512 + (c + 1) * P], w["Wo"][:, c * P:(c + 1) * P],
                          start=(c == 0), stop=(c == 3))
        last.then_inc(sem["layer_out"], 1)


def lha_act(k, act):
    sem, a = k.sem, k.nc.scalar
    for s, sl in enumerate(k.slots):
        act.wait_ge(sem["lha_kshift"], nth(0, s))
        a.activation(sl.a[:, :], sl.a[:, :], ACT.Exp).then_inc(sem["lha_kexp"], 1)
    for s, sl in enumerate(k.slots):
        act.wait_ge(sem["lha_qshift"], nth(0, s))
        a.activation(sl.c[:, :], sl.c[:, :], ACT.Exp).then_inc(sem["lha_qexp"], 1)
    for s, sl in enumerate(k.slots):
        act.wait_ge(sem["lha_v_psum"], nth(0, s))
        a.copy(sl.d[:, :], sl.both).then_inc(sem["lha_v"], 1)
    for s, sl in enumerate(k.slots):
        act.wait_ge(sem["lha_kt_psum"], nth(0, s))
        a.copy(sl.b[:, :], sl.both).then_inc(sem["lha_kt"], 1)
    for j in range(TILES):
        for s, sl in enumerate(k.slots):
            act.wait_ge(sem["lha_oT_psum"], nth(j, s))
            a.copy(sl.c[:, j * 512:(j + 1) * 512], sl.b0).then_inc(sem["lha_oT"], 1)


def lha_dve(k, dve, L):
    sem, v, step = k.sem, k.nc.vector, k.step
    t = []
    for s, sl in enumerate(k.slots):
        dve.wait_ge(sem["projected"], nth(k.projected_at["lha"], s))
        t.append(step(v.tensor_reduce(sl.t[:, 0:16], by64(sl.both), AX.X, ALU.max)))
        dve.wait_ge(step.sem, t[s])
        v.tensor_tensor(by64(sl.a[:, :]), by64(sl.both), spread(sl.t[:, 0:16], 2, SEQ),
                        ALU.subtract).then_inc(sem["lha_kshift"], 1)
    for s, sl in enumerate(k.slots):
        dve.wait_ge(sem["lha_q_psum"], nth(0, s))
        t[s] = step(v.tensor_reduce(sl.t[:, 16:32], by64(sl.both), AX.X, ALU.max))
        dve.wait_ge(step.sem, t[s])
        v.tensor_tensor(by64(sl.c[:, :]), by64(sl.both), spread(sl.t[:, 16:32], 2, 64),
                        ALU.subtract).then_inc(sem["lha_qshift"], 1)
    for s, sl in enumerate(k.slots):
        dve.wait_ge(sem["lha_kexp"], nth(0, s))
        v.tensor_reduce(sl.t[:, 32:48], by64(sl.a[:, :]), AX.X, ALU.add)
        dve.wait_ge(sem["lha_qexp"], nth(0, s))
        t[s] = step(v.tensor_reduce(sl.t[:, 48:64], by64(sl.c[:, :]), AX.X, ALU.add))
    for s, sl in enumerate(k.slots):
        dve.wait_ge(step.sem, t[s])
        t[s] = step(v.reciprocal(sl.t[:, 64:96], sl.t[:, 32:64]))
    for s, sl in enumerate(k.slots):
        dve.wait_ge(step.sem, t[s])
        t[s] = step(v.tensor_scalar(sl.t[:, 96:112], sl.t[:, 80:96], LHA_SCALE, None, ALU.mult))
    for s, sl in enumerate(k.slots):
        dve.wait_ge(step.sem, t[s])
        v.tensor_tensor(by64(sl.c[:, :]), by64(sl.c[:, :]), spread(sl.t[:, 96:112], 2, 64),
                        ALU.mult).then_inc(sem["lha_qn"], 1)
    for s, sl in enumerate(k.slots):
        dve.wait_ge(sem["lha_qT_psum"], nth(0, s))
        v.tensor_tensor(by64(sl.a[:, :]), by64(sl.both), spread(sl.t[:, 64:80], 2, SEQ), ALU.mult).then_inc(sem["lha_qT"], 1)
    for j in range(TILES):
        for s, sl in enumerate(k.slots):
            dve.wait_ge(sem["lha_kv"], nth(j, s))
            v.tensor_tensor(sl.e[:, :].rearrange("p (c e) -> p c e", e=P), sl.both.rearrange("p (c e) -> p c e", e=P),
                            spread(k.const["diag64"], 1, 8), ALU.mult).then_inc(sem["lha_kvm"], 1)
    add_to_x_dve(k, dve, L, "layer_out", k.out_at["lha"], 1)


MLS_HEADS, MLS_D = 8, 16
MLS_EPS = 1e-6


def mls_pe(k, pe, n):
    sem, mm, w = k.sem, k.nc.tensor.matmul, k.w["mls"]
    for s, sl in enumerate(k.slots):
        pe.wait_ge(sem["ln_yT"], nth(n, s))
        for name, out in (("WfT", sl.b0[0:8, 0:256]), ("WiT", sl.b0[0:8, 256:512])):
            for j, src in enumerate((sl.yT, sl.ctxT, sl.ctxT)):
                last = mm(out, w[name][:, 8 * j:8 * j + 8], src[:, :], start=(j == 0), stop=(j == 2))
        last.then_inc(sem["projected"], 1)
    for s, sl in enumerate(k.slots):
        pe.wait_ge(sem["mls_arg"], nth(0, s))
        for b in range(SLOT_BATCHES):
            j = b // HALVES
            cd = (sl.c, sl.d)[j][0:8, (b % HALVES) * 512:(b % HALVES + 1) * 512]
            out = sl.ps[half(b), j, :]
            mm(out, sl.b[0:8, 256 + b * SEQ:256 + (b + 1) * SEQ], k.const["rows_of_8"], start=True, stop=False)
            last = mm(out, k.ones[0:8, 0:SEQ], cd, start=False, stop=True)
        last.then_inc(sem["mls_arg_psum"], 1)
    t = []
    for g in range(4):
        r = slice(32 * g, 32 * g + 32)
        for s, sl in enumerate(k.slots):
            if g:
                pe.wait_ge(k.pe_step.sem, t[s])
            else:
                pe.wait_ge(sem["mls_shift"], nth(0, s))
                pe.wait_ge(sem["mls_qm"], nth(0, s))
            qm = sl.c[:, 0:512].rearrange("p (h t) -> p h t", h=2)
            for b in range(SLOT_BATCHES):
                last = mm(sl.ps[half(b), b // HALVES, g * P:(g + 1) * P].rearrange("p (h t) -> p h t", h=2),
                          sl.ctxT[r, bat(b)], qm[r, :, bat(b)], start=True, stop=True,
                          tile_position=(32 * g, (b % HALVES) * SEQ))
            if g == 3:
                last.then_inc(sem["mls_qk"], 1)
            elif g:
                t[s] = k.pe_step(last)
            else:
                t.append(k.pe_step(last))
    for s, sl in enumerate(k.slots):
        pe.wait_ge(sem["mls_em"], nth(0, s))
        pe.wait_ge(sem["mls_C"], nth(0, s))
        for b in range(SLOT_BATCHES):
            j = b // HALVES
            for h in range(MLS_HEADS):
                mm(sl.b0[half(b), (j * 8 + h) * 17:(j * 8 + h + 1) * 17],
                   sl.e[half(b), j * 512 + h * SEQ:j * 512 + (h + 1) * SEQ], sl.ctxv[half(b), j, h * 17:(h + 1) * 17],
                   start=True, stop=True)
        for j in range(TILES):
            last = k.nc.tensor.transpose(sl.b1[:, 8 * j:8 * j + 8], sl.b[0:8, 768 + j * P:768 + (j + 1) * P], k.ident[0:8, 0:8])
        last.then_inc(sem["mls_out"], 1)


def mls_act(k, act):
    sem, a, w = k.sem, k.nc.scalar, k.w["mls"]
    for s, sl in enumerate(k.slots):
        act.wait_ge(sem["projected"], nth(k.projected_at["mls"], s))
        a.activation(sl.a[0:8, 512:768], sl.b0[0:8, 0:256], ACT.Abs, bias=w["bf"]).then_inc(sem["mls_abs"], 1)
        a.activation(sl.a[0:8, 0:256], sl.b0[0:8, 0:256], ACT.Identity, bias=w["bf"])
        a.activation(sl.a[0:8, 256:512], sl.b0[0:8, 256:512], ACT.Identity, bias=w["bi"])
        act.wait_ge(sem["mls_abs"], nth(0, s))
        now = k.act_step(a.activation(sl.a[0:8, 512:768], sl.a[0:8, 512:768], ACT.Exp, scale=-1.0))
        act.wait_ge(k.act_step.sem, now)
        a.activation(sl.a[0:8, 768:1024], sl.a[0:8, 512:768], ACT.Ln, bias=1.0).then_inc(sem["mls_softplus"], 1)
    for s, sl in enumerate(k.slots):
        act.wait_ge(sem["mls_cum"], nth(0, s))
        a.activation(sl.b[0:8, 768:1024], sl.b[0:8, 768:1024], ACT.Exp, scale=-1.0).then_inc(sem["mls_em"], 1)
    for s, sl in enumerate(k.slots):
        act.wait_ge(sem["mls_shift"], nth(0, s))
        a.activation(sl.e[:, :], sl.e[:, :], ACT.Exp).then_inc(sem["mls_D"], 1)
    for s, sl in enumerate(k.slots):
        act.wait_ge(sem["mls_out"], nth(0, s))
        a.activation(sl.t[:, 0:16], sl.b0[:, 0:272].rearrange("p (g e) -> p g e", e=17)[:, :, 16], ACT.Abs)
        a.activation(sl.t[:, 16:32], sl.b1[:, 0:16], ACT.Copy, bias=MLS_EPS).then_inc(sem["mls_sum"], 1)
    for s, sl in enumerate(k.slots):
        act.wait_ge(sem["mls_h"], nth(0, s))
        a.square(sl.d[:, 0:256], sl.c[:, 0:256]).then_inc(sem["mls_sq"], 1)


def mls_dve(k, dve, L, n):
    sem, v, w, step = k.sem, k.nc.vector, k.w["mls"], k.step
    t = []
    for s, sl in enumerate(k.slots):
        dve.wait_ge(sem["mls_softplus"], nth(0, s))
        t.append(step(v.scalar_tensor_tensor(out=sl.a[0:8, 0:256], in0=sl.a[0:8, 0:256], scalar=0.0,
                                           in1=sl.a[0:8, 768:1024], op0=ALU.min, op1=ALU.subtract)))
        dve.wait_ge(step.sem, t[s])
        t[s] = step(v.tensor_tensor_scan(sl.b[0:8, 0:256], k.const["not_first"], sl.a[0:8, 0:256], 0.0,
                                             ALU.mult, ALU.add))
        dve.wait_ge(step.sem, t[s])
        t[s] = step(v.tensor_tensor(sl.b[0:8, 256:512], sl.a[0:8, 256:512], sl.b[0:8, 0:256], ALU.subtract))
        dve.wait_ge(step.sem, t[s])
        t[s] = step(v.tensor_tensor_scan(sl.b[0:8, 512:768], k.const["first_neg"], sl.b[0:8, 256:512], 0.0,
                                             ALU.add, ALU.max))
        dve.wait_ge(step.sem, t[s])
        v.tensor_tensor(sl.b[0:8, 768:1024], sl.b[0:8, 0:256], sl.b[0:8, 512:768], ALU.add).then_inc(sem["mls_cum"], 1)
        for j, dst in enumerate((sl.c, sl.d)):
            last = v.tensor_tensor(dst[0:8, :].rearrange("p (b h t) -> p b h t", b=HALVES, h=MLS_HEADS),
                                   spread(sl.b[0:8, 512 + j * P:512 + (j + 1) * P].rearrange("p (b t) -> p b t", b=HALVES), 2, MLS_HEADS),
                                   spread(k.const["minus_delta8"].rearrange("p (h t) -> p h t", h=MLS_HEADS), 1, HALVES),
                                   ALU.mult)
        last.then_inc(sem["mls_arg"], 1)
    for s, sl in enumerate(k.slots):
        dve.wait_ge(sem["mls_arg_psum"], nth(0, s))
        v.scalar_tensor_tensor(out=by64(sl.e[:, :]), in0=by64(sl.both), scalar=0.0,
                               in1=spread(k.const["causal_neg"], 1, 16), op0=ALU.min, op1=ALU.add).then_inc(sem["mls_shift"], 1)
    for s, sl in enumerate(k.slots):
        v.tensor_tensor(sl.c[:, 0:512].rearrange("p (h t) -> p h t", h=2),
                        spread(sl.yT[:, :], 1, 2), spread(k.const["head_of_2"], 2, SLOT_TOKENS),
                        ALU.mult).then_inc(sem["mls_qm"], 1)
    for s, sl in enumerate(k.slots):
        dve.wait_ge(sem["mls_qk"], nth(0, s))
        dve.wait_ge(sem["mls_D"], nth(0, s))
        v.scalar_tensor_tensor(out=sl.e[:, :], in0=sl.both, scalar=MLS_D ** -0.5, in1=sl.e[:, :],
                               op0=ALU.mult, op1=ALU.mult).then_inc(sem["mls_C"], 1)
    for s, sl in enumerate(k.slots):
        heads = sl.b0[:, 0:272].rearrange("p (g e) -> p g e", e=17)
        h = sl.c[:, 0:256].rearrange("p (g e) -> p g e", e=MLS_D)
        dve.wait_ge(sem["mls_sum"], nth(0, s))
        t[s] = step(v.scalar_tensor_tensor(out=sl.t[:, 16:32], in0=sl.t[:, 0:16], scalar=MLS_EPS, in1=sl.t[:, 16:32],
                                           op0=ALU.add, op1=ALU.max))
        dve.wait_ge(step.sem, t[s])
        t[s] = step(v.reciprocal(sl.t[:, 32:48], sl.t[:, 16:32]))
        dve.wait_ge(step.sem, t[s])
        t[s] = step(v.tensor_tensor(h, heads[:, :, 0:16], spread(sl.t[:, 32:48], 2, MLS_D), ALU.mult))
        dve.wait_ge(step.sem, t[s])
        t[s] = step(v.tensor_reduce(sl.t[:, 48:64], h, AX.X, ALU.add))
        dve.wait_ge(step.sem, t[s])
        v.scalar_tensor_tensor(out=h, in0=spread(sl.t[:, 48:64], 2, MLS_D), scalar=-1.0 / MLS_D, in1=h,
                               op0=ALU.mult, op1=ALU.add).then_inc(sem["mls_h"], 1)
    for s, sl in enumerate(k.slots):
        c = sl.c[:, 0:256].rearrange("p (t c) -> p t c", t=TILES)
        dve.wait_ge(sem["mls_sq"], nth(0, s))
        v.tensor_reduce(sl.t[:, 80:96], sl.d[:, 0:256].rearrange("p (g e) -> p g e", e=MLS_D), AX.X,
                        ALU.add).then_inc(sem["mls_var"], 1)
        t[s] = step(v.tensor_tensor(c, c, spread(w["norm"], 1, TILES), ALU.mult))
    for s, sl in enumerate(k.slots):
        h = sl.c[:, 0:256].rearrange("p (g e) -> p g e", e=MLS_D)
        dve.wait_ge(step.sem, t[s])
        dve.wait_ge(sem["mls_rstd"], nth(0, s))
        t[s] = step(v.tensor_tensor(h, h, spread(sl.t[:, 96:112], 2, MLS_D), ALU.mult))
        dve.wait_ge(step.sem, t[s])
        v.tensor_tensor(sl.x[:, :, :], sl.x[:, :, :], sl.c[:, 0:256].rearrange("p (t c) -> p t c", t=TILES),
                        ALU.add).then_inc(sem["x_updated"], 1)
        statistics_dve(k, dve, L + 1, s, sl)


def mls_pool(k, pool):
    g = k.nc.gpsimd
    for s, sl in enumerate(k.slots):
        pool.wait_ge(k.sem["mls_var"], nth(0, s))
        now = k.pool_step(g.tensor_scalar(sl.t[:, 96:112], sl.t[:, 80:96], 1.0 / MLS_D, EPS, ALU.mult, ALU.add))
        pool.wait_ge(k.pool_step.sem, now)
        g.tensor_tensor(sl.t[:, 96:112], sl.t[:, 96:112], k.minus_half, ALU.pow).then_inc(k.sem["mls_rstd"], 1)




def by_batch(ap):
    return ap.rearrange("p (b t) -> p b t", b=SLOT_BATCHES)


def chunk0(ap, shift=0):
    return by_batch(ap)[:, :, shift:CHUNK + shift]


def ttt_pe(k, pe, n):
    sem, mm, w = k.sem, k.nc.tensor.matmul, k.w["ttt"]

    for s, sl in enumerate(k.slots):
        pe.wait_ge(sem["ttt_z"], nth(0, s))
        pe.wait_ge(sem["ln_yT"], nth(n, s))
        for j in range(TILES):
            last = k.nc.tensor.transpose(sl.b0[:, tok(j)], sl.a[:, tok(j)], k.ident)
        last.then_inc(sem["ttt_zT_psum"], 1)
    for s, sl in enumerate(k.slots):
        pe.wait_ge(sem["ttt_xnT"], nth(0, s))
        nxt, z = sl.b[:, 0:128], sl.b[:, 128:256]
        mm(sl.b0[:, 0:128], nxt, w["WpT"], start=True, stop=True)
        mm(sl.b0[:, 128:256], w["WpT"], nxt, start=True, stop=True)
        mm(sl.b0[:, 256:384], z, k.ident, start=True, stop=True)
        mm(sl.b0[:, 384:400], z, w["BT"], start=True, stop=True).then_inc(sem["ttt_p1"], 1)
    for s, sl in enumerate(k.slots):
        pe.wait_ge(sem["ttt_s1"], nth(0, s))
        mm(sl.b1[:, 0:16], sl.c[:, 128:256], w["A"], start=True, stop=True).then_inc(sem["ttt_p2"], 1)
    for s, sl in enumerate(k.slots):
        pe.wait_ge(sem["ttt_s2"], nth(0, s))
        mm(sl.b0[0:64, 0:P], sl.e[:, 128:192], sl.c[:, 0:128], start=True, stop=True)
        mm(sl.b0[:, 128:192], sl.c[:, 256:384], sl.e[:, 192:256], start=True, stop=True).then_inc(sem["ttt_d"], 1)
    for s, sl in enumerate(k.slots):
        pe.wait_ge(sem["ttt_sq"], nth(0, s))
        mm(sl.b1[:, 0:4], k.ones[0:64, :], sl.t[0:64, 4:8], start=True, stop=False)
        mm(sl.b1[:, 0:4], k.ones, sl.t[:, 0:4], start=False, stop=True).then_inc(sem["ttt_norm"], 1)
    for s, sl in enumerate(k.slots):
        pe.wait_ge(sem["ttt_eff"], nth(0, s))
        mm(sl.b0[0:64, 0:256], sl.e[:, 0:64], sl.yT[:, :], start=True, stop=True)
        mm(sl.b0[0:16, 256:512], w["BT"], sl.yT[:, :], start=True, stop=True).then_inc(sem["ttt_mid_psum"], 1)
    for s, sl in enumerate(k.slots):
        pe.wait_ge(sem["ttt_mid"], nth(0, s))
        for j in range(TILES):
            mm(sl.b1[:, tok(j)], sl.yT[:, tok(j)], w["WbT"], start=True, stop=False)
            mm(sl.b1[:, tok(j)], sl.a[0:16, 256 + j * P:256 + (j + 1) * P], w["AT"], start=False, stop=False)
            last = mm(sl.b1[:, tok(j)], sl.a[0:64, tok(j)], sl.d[0:64, 0:P], start=False, stop=True)
        last.then_inc(sem["layer_out"], 1)


def ttt_act(k, act):
    sem, a, w = k.sem, k.nc.scalar, k.w["ttt"]
    for s, sl in enumerate(k.slots):
        act.wait_ge(sem["ttt_zT_psum"], nth(0, s))
        a.copy(by_batch(sl.b[:, 128:256]), chunk0(sl.yT[:, :]))
        a.activation(by_batch(sl.b[:, 0:128]), chunk0(sl.b0[:, 0:256], 1), ACT.Identity, bias=w["beta"],
                     scale=w["gamma"]).then_inc(sem["ttt_xnT"], 1)
    for s, sl in enumerate(k.slots):
        act.wait_ge(sem["ttt_p1"], nth(0, s))
        a.copy(sl.c[:, 0:400], sl.b0[:, 0:400]).then_inc(sem["ttt_s1"], 1)
    lr = TTT_LR * TTT_SCALING
    for s, sl in enumerate(k.slots):
        act.wait_ge(sem["ttt_d"], nth(0, s))
        a.activation(sl.e[:, 64:128], sl.b0[:, 128:192], ACT.Square, scale=lr)
        a.activation(sl.d[0:64, P:2 * P], sl.b0[0:64, 0:P], ACT.Square, scale=lr,
                     accum_out=sl.t[0:64, 24:25]).then_inc(sem["ttt_squares"], 1)
        a.activation(sl.d[0:64, 0:P], sl.b0[0:64, 0:P], ACT.Copy, scale=lr)
        a.activation(sl.e[:, 0:64], sl.b0[:, 128:192], ACT.Copy, scale=lr).then_inc(sem["ttt_raw"], 1)


def ttt_dve(k, dve, L, n):
    sem, v, w, step = k.sem, k.nc.vector, k.w["ttt"], k.step
    t = []
    for s, sl in enumerate(k.slots):
        dve.wait_ge(sem["ln_y"], nth(n, s))
        for j in range(TILES):
            last = v.bn_stats(sl.stats[:, j, :], sl.y[:, j, :])
        t.append(step(last))
        dve.wait_ge(step.sem, t[s])
        for j in range(TILES):
            last = v.bn_aggr(sl.mv[:, j, :], sl.stats[:, j, :])
        last.then_inc(sem["inner_stats"], 1)
    for s, sl in enumerate(k.slots):
        dve.wait_ge(sem["inner_rstd"], nth(k.inner_at["ttt"], s))
        for j in range(TILES):
            last = v.tensor_scalar(sl.a[:, tok(j)], sl.y[:, j, :], sl.mv[:, j, 0:1], sl.rstd[:, j:j + 1],
                                   ALU.subtract, ALU.mult)
        last.then_inc(sem["ttt_z"], 1)
    for s, sl in enumerate(k.slots):
        own = by_batch(k.const["batch_rows"])
        dve.wait_ge(sem["ttt_s1"], nth(0, s))
        v.tensor_tensor(by_batch(sl.e[:, 128:192]), spread(sl.c[:, 384:400], 1, 4), own, ALU.mult)
        dve.wait_ge(sem["ttt_p2"], nth(0, s))
        v.tensor_tensor(by_batch(sl.e[:, 192:256]), spread(sl.b1[:, 0:16], 1, 4), own, ALU.mult).then_inc(sem["ttt_s2"], 1)
    for s, sl in enumerate(k.slots):
        dve.wait_ge(sem["ttt_squares"], nth(0, s))
        v.tensor_reduce(sl.t[:, 0:4], by_batch(sl.e[:, 64:128]), AX.X, ALU.add)
        v.tensor_scalar(sl.t[0:64, 4:8], k.const["batch_of_rank"], sl.t[0:64, 24:25], None, ALU.mult).then_inc(sem["ttt_sq"], 1)
    for s, sl in enumerate(k.slots):
        dve.wait_ge(sem["ttt_norm"], nth(0, s))
        v.tensor_copy(sl.t[:, 8:12], sl.b1[:, 0:4]).then_inc(sem["ttt_nsq"], 1)
    for s, sl in enumerate(k.slots):
        dve.wait_ge(sem["ttt_root"], nth(0, s))
        t[s] = step(v.reciprocal(sl.t[:, 16:20], sl.t[:, 12:16]))
        dve.wait_ge(step.sem, t[s])
        t[s] = step(v.tensor_scalar(sl.t[:, 20:24], sl.t[:, 16:20], -TTT_CLIP, -1.0, ALU.mult, ALU.max))
        dve.wait_ge(step.sem, t[s])
        dve.wait_ge(sem["ttt_raw"], nth(0, s))
        e = by_batch(sl.e[:, 0:64])
        t[s] = step(v.tensor_tensor(sl.t[0:64, 28:32], sl.t[0:64, 20:24], k.const["batch_of_rank"], ALU.mult))
        v.tensor_tensor(e, e, spread(sl.t[:, 20:24], 2, RANK), ALU.mult)
        dve.wait_ge(step.sem, t[s])
        t[s] = step(v.tensor_reduce(sl.t[0:64, 25:26], sl.t[0:64, 28:32], AX.X, ALU.add))
        dve.wait_ge(step.sem, t[s])
        v.tensor_tensor(e, spread(w["BT"], 1, 4), e, ALU.add)
        v.scalar_tensor_tensor(out=sl.d[0:64, 0:P], in0=sl.d[0:64, 0:P], scalar=sl.t[0:64, 25:26], in1=w["AT4"],
                               op0=ALU.mult, op1=ALU.add).then_inc(sem["ttt_eff"], 1)
    for s, sl in enumerate(k.slots):
        dve.wait_ge(sem["ttt_mid_psum"], nth(0, s))
        v.tensor_tensor(sl.a[0:16, 256:512], sl.b0[0:16, 256:512], k.const["first_chunk"], ALU.mult)
        v.tensor_tensor(sl.a[0:64, 0:256], sl.b0[0:64, 0:256], k.const["second_chunk"], ALU.mult).then_inc(sem["ttt_mid"], 1)
    add_to_x_dve(k, dve, L, "layer_out", k.out_at["ttt"], 1)


def ttt_pool(k, pool):
    g = k.nc.gpsimd
    for s, sl in enumerate(k.slots):
        pool.wait_ge(k.sem["ttt_nsq"], nth(0, s))
        now = k.pool_step(g.tensor_tensor(sl.t[:, 12:16], sl.t[:, 8:12], k.half[:, 0:4], ALU.pow))
        pool.wait_ge(k.pool_step.sem, now)
        g.tensor_scalar(sl.t[:, 12:16], sl.t[:, 12:16], 1e-6, None, ALU.add).then_inc(k.sem["ttt_root"], 1)


def dia_pe(k, pe, L):
    sem, mm, w = k.sem, k.nc.tensor.matmul, k.w["dia"]
    for s, sl in enumerate(k.slots):
        if L:
            pe.wait_ge(sem["x_updated"], nth(L - 1, s))
        mm(sl.b0[:, 0:256], w["WvT"], sl.ctxT[:, :], start=True, stop=True).then_inc(sem["projected"], 1)
    for s, sl in enumerate(k.slots):
        pe.wait_ge(sem["dia_vT"], nth(0, s))
        for j in range(TILES):
            last = mm(sl.b1[:, tok(j)], sl.a[:, tok(j)], w["WoT"], start=True, stop=True)
        last.then_inc(sem["layer_out"], 1)


def dia_act(k, act):
    for s, sl in enumerate(k.slots):
        act.wait_ge(k.sem["projected"], nth(k.projected_at["dia"], s))
        k.nc.scalar.activation(sl.a[:, 0:256], sl.b0[:, 0:256], ACT.Identity, bias=k.w["dia"]["bv"]).then_inc(k.sem["dia_vT"], 1)


LAYERS = ("bin", "mha", "moe", "lin", "one", "tree", "lha", "mls", "fst", "ttt", "dia", "ffn")
NORMALISED = [name for name in LAYERS if name != "dia"]
PROJECTED = [name for name in LAYERS if name in ("mha", "lin", "one", "tree", "lha", "mls", "dia")]
OUT = [name for name in LAYERS if name not in ("moe", "mls", "ffn")]
INNER = [name for name in LAYERS if name in ("mha", "lin", "ttt")]
BIASED = [name for name in LAYERS if name in ("lin", "tree", "lha", "dia")]
GATED = [name for name in LAYERS if name in ("moe", "fst", "ffn")]


def build(nc, xg, ctxTg, ctxvg, packs, where, out):
    ctx = ExitStack()
    with ctx:
        k = Kern()
        k.nc = nc
        k.slots = [Slot(nc, ctx, s) for s in range(SLOTS)]
        weights, k.w = {}, {}
        for name, dram in packs.items():
            weights[name] = ctx.enter_context(nc.sbuf_tensor(f"w_{name}", [P, dram.shape[1]], F32))
            k.w[name] = {piece: weights[name][0:p, at:at + n] for piece, (p, at, n) in where[name].items()}
        k.const = k.w["const"]
        k.ident, k.ones = k.const["ident"], k.const["ones"]
        powers = ctx.enter_context(nc.sbuf_tensor("powers", [P, 32], F32))
        k.minus_half, k.half = powers[:, 0:16], powers[:, 16:32]
        w_loaded = {name: ctx.enter_context(nc.semaphore(f"{name}_weights_loaded")) for name in packs}
        s_set = ctx.enter_context(nc.semaphore("buffers_set"))
        bin_step = ctx.enter_context(nc.semaphore("bin_step"))
        cleared = [ctx.enter_context(nc.semaphore(name)) for name in SIGNALS]
        k.sem = dict(zip(SIGNALS, cleared))
        next_loaded = ctx.enter_context(nc.semaphore("next_loaded"))
        x_stored = [ctx.enter_context(nc.semaphore(f"x_stored{s}")) for s in range(SLOTS)]
        cleared += [next_loaded] + x_stored
        first_loaded = ctx.enter_context(nc.semaphore("first_loaded"))
        k.projected_at = {name: n for n, name in enumerate(PROJECTED)}
        k.out_at = {name: n for n, name in enumerate(OUT)}
        k.normalised_at = {L: NORMALISED.index(name) for L, name in enumerate(LAYERS) if name in NORMALISED}
        k.inner_at = {name: n for n, name in enumerate(INNER)}
        k.moe_first = {"ffn": MOE_NETS if "moe" in LAYERS else 0}

        with nc.Block() as block:
            @block.sync
            def _(sp):
                early = [name for name in packs if name in ("const", "bin")]
                for name in early:
                    sp.dma_start(weights[name][:, :], packs[name]).then_inc(w_loaded[name], 16)
                last = slice((GROUPS - 1) * P, GROUPS * P)
                for s, sl in enumerate(k.slots):
                    sp.dma_start(sl.x[:, :, :], xg[last][:, s]).then_inc(first_loaded, 16)
                for s, sl in enumerate(k.slots):
                    sp.dma_start(sl.ctxT[:, :], ctxTg[last][:, s]).then_inc(first_loaded, 16)
                for s, sl in enumerate(k.slots):
                    sp.dma_start(sl.ctxv[:, :, :], ctxvg[last][:, s]).then_inc(first_loaded, 16)
                for name in packs:
                    if name not in early:
                        sp.dma_start(weights[name][:, :], packs[name]).then_inc(w_loaded[name], 16)
                sp.wait_ge(first_loaded, 3 * 16 * SLOTS)

            @block.gpsimd
            def _(pool):
                nc.gpsimd.memset(k.minus_half, -0.5)
                nc.gpsimd.memset(k.half, 0.5)
                for sl in k.slots:
                    nc.gpsimd.memset(sl.g[:, :], 0.0)
                    nc.gpsimd.memset(sl.w[:, :, :], 1.0)
                    last = nc.gpsimd.memset(sl.w6[:, :, :], 1.0 / FFN_SHARED)
                last.then_inc(s_set, 1)
                pool.wait_ge(s_set, 1)

            @block.scalar
            def _(act):
                if "bin" in LAYERS:
                    act.wait_ge(w_loaded["bin"], 16)
                    for name in ("bq", "bk", "bv"):
                        last = nc.scalar.activation(bin_sign(k, name), k.w["bin"][name], ACT.Sign)
                    last.then_inc(bin_step, 1)

            @block.vector
            def _(dve):
                if "bin" in LAYERS:
                    dve.wait_ge(w_loaded["bin"], 16)
                    dve.wait_ge(bin_step, 1)
                    for name in ("bq", "bk", "bv"):
                        s = bin_sign(k, name)
                        last = nc.vector.tensor_tensor(s, s, k.w["bin"][name], ALU.subtract)
                    last.then_inc(bin_step, 1)
                    dve.wait_ge(bin_step, 2)
                    for name in ("bq", "bk", "bv"):
                        last = nc.vector.tensor_tensor(k.w["bin"][name], bin_sign(k, name), k.w["bin"][name], ALU.add)
                    last.then_inc(bin_step, 1)
                    dve.wait_ge(bin_step, 3)

        with nc.Fori(0, GROUPS) as group:
            with nc.Block() as block:
                @block.sync
                def _(sp):
                    def rows_of(dram):
                        return dram[bass.ds(group * P, P)]
                    if "dia" in LAYERS:
                        sp.wait_ge(k.sem["layer_out"], nth(k.out_at["dia"], SLOTS - 1))
                    for s, sl in enumerate(k.slots):
                        sp.dma_start(sl.ctxT[:, :], rows_of(ctxTg)[:, s]).then_inc(next_loaded, 16)
                        sp.dma_start(sl.ctxv[:, :, :], rows_of(ctxvg)[:, s]).then_inc(next_loaded, 16)
                    for s, sl in enumerate(k.slots):
                        sp.wait_ge(k.sem["x_updated"], nth(len(LAYERS) - 1, s))
                        sp.dma_start(rows_of(out)[:, s], sl.x[:, :, :]).then_inc(x_stored[s], 16)
                    for s, sl in enumerate(k.slots):
                        sp.wait_ge(x_stored[s], 16)
                        sp.dma_start(sl.x[:, :, :], rows_of(xg)[:, s]).then_inc(next_loaded, 16)
                    sp.wait_ge(next_loaded, 3 * 16 * SLOTS)

                @block.tensor
                def _(pe):
                    k.pe_step = Steps(k.sem["pe_step"])
                    pe.wait_ge(w_loaded["const"], 16)
                    n = 0
                    for L, name in enumerate(LAYERS):
                        if name == "mha":
                            pe.wait_ge(w_loaded[name], 16)
                            mha_context_pe(k, pe, L)
                        if name == "one":
                            pe.wait_ge(w_loaded[name], 16)
                            one_context_pe(k, pe, L)
                        if name != "dia":
                            normalise_pe(k, pe, n)
                        pe.wait_ge(w_loaded[name], 16)
                        if name == "bin":
                            bin_pe(k, pe)
                        if name == "mha":
                            mha_pe(k, pe, n)
                        if name == "moe":
                            moe_pe(k, pe, n, GATED.index(name))
                        if name == "lin":
                            lin_pe(k, pe, n)
                        if name == "one":
                            one_pe(k, pe, n)
                        if name == "tree":
                            tree_pe(k, pe, n)
                        if name == "lha":
                            lha_pe(k, pe, n)
                        if name == "mls":
                            mls_pe(k, pe, n)
                        if name == "fst":
                            fst_pe(k, pe, n, GATED.index(name))
                        if name == "ttt":
                            ttt_pe(k, pe, n)
                        if name == "dia":
                            dia_pe(k, pe, L)
                        if name == "ffn":
                            ffn_pe(k, pe, n, GATED.index(name))
                        n += name != "dia"

                @block.scalar
                def _(act):
                    k.act_step = Steps(k.sem["act_step"])
                    n = 0
                    for name in LAYERS:
                        if name != "dia":
                            normalise_act(k, act, n)
                        act.wait_ge(w_loaded[name], 16)
                        if name == "bin":
                            bin_act(k, act)
                        if name == "mha":
                            mha_act(k, act)
                        if name == "moe":
                            moe_act(k, act, GATED.index(name))
                        if name == "lin":
                            lin_act(k, act)
                        if name == "one":
                            one_act(k, act)
                        if name == "tree":
                            tree_act(k, act)
                        if name == "lha":
                            lha_act(k, act)
                        if name == "mls":
                            mls_act(k, act)
                        if name == "fst":
                            fst_act(k, act, GATED.index(name))
                        if name == "ttt":
                            ttt_act(k, act)
                        if name == "dia":
                            dia_act(k, act)
                        if name == "ffn":
                            ffn_act(k, act, GATED.index(name))
                        n += name != "dia"

                @block.gpsimd
                def _(pool):
                    k.pool_step = Steps(k.sem["pool_step"])
                    n = 0
                    for L, name in enumerate(LAYERS):
                        if name != "dia":
                            rstd_pool(k, pool, "ln_stats", "ln_rstd", n, TILES)
                        if name in BIASED:
                            pool.wait_ge(w_loaded[name], 16)
                            bias_pool(k, pool, L, name)
                        if name == "mha":
                            rstd_pool(k, pool, "inner_stats", "inner_rstd", k.inner_at["mha"], 2 * TILES)
                        if name == "lin":
                            rstd_pool(k, pool, "inner_stats", "inner_rstd", k.inner_at["lin"], TILES)
                        if name == "mls":
                            mls_pool(k, pool)
                        if name == "ttt":
                            rstd_pool(k, pool, "inner_stats", "inner_rstd", k.inner_at["ttt"], TILES)
                            ttt_pool(k, pool)
                        n += name != "dia"

                @block.vector
                def _(dve):
                    k.step = Steps(k.sem["dve_step"])
                    dve.wait_ge(w_loaded["const"], 16)
                    n = 0
                    for L, name in enumerate(LAYERS):
                        if name != "dia":
                            normalise_dve(k, dve, L, n)
                        dve.wait_ge(w_loaded[name], 16)
                        if name == "bin":
                            bin_dve(k, dve, L, n)
                        if name == "mha":
                            mha_dve(k, dve, L)
                        if name == "moe":
                            moe_dve(k, dve, L, GATED.index(name))
                        if name == "lin":
                            lin_dve(k, dve, L)
                        if name == "one":
                            one_dve(k, dve, L)
                        if name == "tree":
                            tree_dve(k, dve, L)
                        if name == "lha":
                            lha_dve(k, dve, L)
                        if name == "mls":
                            mls_dve(k, dve, L, n)
                        if name == "fst":
                            fst_dve(k, dve, L, GATED.index(name))
                        if name == "ttt":
                            ttt_dve(k, dve, L, n)
                        if name == "dia":
                            add_to_x_dve(k, dve, L, "layer_out", k.out_at["dia"], 1)
                        if name == "ffn":
                            ffn_dve(k, dve, L, GATED.index(name))
                        n += name != "dia"
            nc.sync.sem_clear(range(cleared[0].num, cleared[-1].num + 1))
            nc.all_engine_barrier()


def bin_sign(k, name):
    sl = k.slots[0]
    return {"bq": sl.t[:, 0:1], "bk": sl.t[:, 1:2], "bv": sl.a[:, 0:P]}[name]


def by_group(a, width):
    return np.ascontiguousarray(a.reshape(GROUPS, SLOTS, TILES, P, width).transpose(0, 3, 1, 2, 4)).reshape(
        GROUPS * P, SLOTS, TILES, width)


def following(a):
    return np.ascontiguousarray(np.roll(a, -P, axis=0))


def kernel(**inputs):
    import concourse.bacc as bacc
    from concourse.bass_utils import run_bass_kernel_spmd

    i = {name: np.asarray(a) for name, a in inputs.items()}
    nc = bacc.Bacc("TRN2", target_bir_lowering=False, num_devices=1)
    arrays = {"x": following(by_group(i["x"].reshape(TOKENS, D), D))}
    c = i["ctx_1024"].reshape(TOKENS, D)
    arrays["ctxT"] = following(np.ascontiguousarray(
        c.reshape(GROUPS, SLOTS, SLOT_TOKENS, D).transpose(0, 3, 1, 2)).reshape(GROUPS * P, SLOTS, SLOT_TOKENS))
    v = np.ones((TOKENS, 8, 17), np.float32)
    v[:, :, 0:16] = c.reshape(TOKENS, 8, 16)
    arrays["ctxv"] = following(by_group(v.reshape(TOKENS, CTXV), CTXV))
    where, packs = {}, {}
    for name, parts in pieces(i).items():
        if name == "const" or name in LAYERS:
            arrays[f"w_{name}"], where[name] = pack(parts)

    def declared(name, shape, kind):
        return nc.dram_tensor(f"{name}_dram", shape, F32, kind=kind).ap()

    drams = {name: declared(name, a.shape, "ExternalInput") for name, a in arrays.items()}
    out = declared("out", arrays["x"].shape, "ExternalOutput")
    build(nc, drams["x"], drams["ctxT"], drams["ctxv"], {n: drams[f"w_{n}"] for n in where}, where, out)
    r = run_bass_kernel_spmd(nc, [{f"{name}_dram": a for name, a in arrays.items()}], core_ids=[0])
    y = r.results[0]["out_dram"].reshape(GROUPS, P, SLOTS, TILES, D).transpose(0, 2, 3, 1, 4)
    return np.ascontiguousarray(y).reshape(BATCHES, SEQ, D)
```
